# Optimizing a Trainium2 kernel written in Bass

```python
import numpy as np
import jax
import jax.numpy as jnp

def _softmax(x, axis=-1):
    return jax.nn.softmax(x, axis=axis)

def _gelu(x):
    return jax.nn.gelu(x, approximate=True)

def _silu(x):
    return jax.nn.silu(x)

def _sigmoid(x):
    return jax.nn.sigmoid(x)

def _layernorm(x, axis=-1, eps=1e-05):
    m = jnp.mean(x, axis=axis, keepdims=True)
    v = jnp.var(x, axis=axis, keepdims=True)
    return (x - m) / jnp.sqrt(v + eps)

def _scatter_add(tgt, idx, src, axis=0):
    return tgt.at[idx].add(src)

def _segment_sum(src, seg, n):
    return jax.ops.segment_sum(src, seg, n)
kernel_name = 'mk_decoder_preln_d1_seqx_r8_0a733c'

def setup_inputs(seed: int=0):
    np.random.seed(seed)
    _w = jnp.asarray

    def _rec_inputs():
        import jax
        import jax.numpy as jnp
        _rk = jax.random.key(seed)
        x = -0.0003929 + 0.9999 * jax.random.normal(jax.random.fold_in(_rk, 1), (32, 64, 512), jnp.float32)
        _lenS = 64 - jax.random.randint(jax.random.fold_in(_rk, 7), (32,), 0, max(1, 64 // 4) + 1, jnp.int32)
        _lenS2 = 64 - jax.random.randint(jax.random.fold_in(_rk, 8), (32,), 0, max(1, 64 // 4) + 1, jnp.int32)
        _ctx_4096P = jax.random.normal(jax.random.fold_in(_rk, 11), (32, 16, 512), jnp.float32)
        _ctx_4096c = jax.random.dirichlet(jax.random.fold_in(_rk, 511), 0.3 * jnp.ones((16,), jnp.float32), (32, 64))
        _ctx_4096t = jnp.einsum('bsk,bkd->bsd', _ctx_4096c, _ctx_4096P)
        _ctx_4096t = _ctx_4096t * jax.lax.rsqrt(jnp.mean(jnp.square(_ctx_4096t)) + 1e-12) * 0.953939
        ctx_4096 = 2.81802e-05 + 1.00001 * (_ctx_4096t + 0.3 * jax.random.normal(jax.random.fold_in(_rk, 611), (32, 64, 512), jnp.float32))
        pos_BxS2 = jnp.broadcast_to(jnp.arange(64, dtype=jnp.int32), (32, 64))
        _validS = jnp.arange(64)[None, :] < _lenS[:, None]
        _validS2 = jnp.arange(64)[None, :] < _lenS2[:, None]
        _causal = jnp.tril(jnp.ones((64, 64), dtype=bool))
        mask_BxSxS2_ik0 = jnp.where(jnp.broadcast_to(_validS2[:, None, :], (32, 64, 64)), 0, 1).astype(jnp.int32)
        return (x, ctx_4096, pos_BxS2, mask_BxSxS2_ik0)
    x, ctx_4096, pos_BxS2, mask_BxSxS2_ik0 = _rec_inputs()

    def _L0_attn_setup():
        import jax, jax.numpy as jnp
        import numpy as np
        HIDDEN = 512
        HEADS = 32
        D_K = HIDDEN // HEADS
        key = jax.random.key(seed)
        ks = jax.random.split(key, 5)
        scale = 1.0 / np.sqrt(HIDDEN)
        x = jax.random.normal(ks[0], (2, 256, HIDDEN), dtype=jnp.float32)
        w_q = jax.random.uniform(ks[1], (HIDDEN, HIDDEN), jnp.float32, -scale, scale)
        w_k = jax.random.uniform(ks[2], (HIDDEN, HIDDEN), jnp.float32, -scale, scale)
        w_v = jax.random.uniform(ks[3], (HIDDEN, HIDDEN), jnp.float32, -scale, scale)
        w_o = jax.random.uniform(ks[4], (HIDDEN, HIDDEN), jnp.float32, -scale, scale)
        return {'x': x, 'w_q': w_q, 'w_k': w_k, 'w_v': w_v, 'w_o': w_o}
    _L0_attn_all = _L0_attn_setup()
    _L0_attn_in = {k: v for k, v in _L0_attn_all.items() if k in ('w_q', 'w_k', 'w_v', 'w_o')}
    del _L0_attn_all

    def _L0_xattn_setup():
        import jax, jax.numpy as jnp
        import numpy as np
        B, S, E = (2, 256, 512)
        H, KVH, D = (32, 8, 128)
        GROUPS = H // KVH
        MAX_POS = 512
        ROPE_THETA = 10000.0

        def _rope_tables(max_pos, dim, theta):
            inv_freq = 1.0 / theta ** (jnp.arange(0, dim, 2, dtype=jnp.float32) / dim)
            t = jnp.arange(max_pos, dtype=jnp.float32)
            freqs = jnp.einsum('i,j->ij', t, inv_freq)
            emb = jnp.concatenate([freqs, freqs], axis=-1)
            return (jnp.cos(emb), jnp.sin(emb))

        def _rotate_half(x):
            x1, x2 = (x[..., :x.shape[-1] // 2], x[..., x.shape[-1] // 2:])
            return jnp.concatenate([-x2, x1], axis=-1)
        key = jax.random.key(seed)
        ks = jax.random.split(key, 8)
        scale_w = 1.0 / np.sqrt(E)
        query = jax.random.normal(ks[0], (B, S, E), dtype=jnp.float32)
        k_in = jax.random.normal(ks[1], (B, S, E), dtype=jnp.float32)
        v_in = jax.random.normal(ks[2], (B, S, E), dtype=jnp.float32)
        position_ids = jnp.broadcast_to(jnp.arange(S, dtype=jnp.int64), (B, S))
        src_mask = jnp.tril(jnp.ones((S, S), dtype=jnp.int32))
        src_mask = jnp.broadcast_to(src_mask, (B, S, S))
        Wq = jax.random.normal(ks[3], (E, H * D), dtype=jnp.float32) * scale_w
        Wk = jax.random.normal(ks[4], (E, KVH * D), dtype=jnp.float32) * scale_w
        Wv = jax.random.normal(ks[5], (E, KVH * D), dtype=jnp.float32) * scale_w
        Wo = jax.random.normal(ks[6], (H * D, E), dtype=jnp.float32) * scale_w
        return {'query': query, 'key': k_in, 'value': v_in, 'position_ids': position_ids, 'src_mask': src_mask, 'Wq': Wq, 'Wk': Wk, 'Wv': Wv, 'Wo': Wo}
    _L0_xattn_all = _L0_xattn_setup()
    _L0_xattn_in = {k: v for k, v in _L0_xattn_all.items() if k in ('Wq', 'Wk', 'Wv', 'Wo')}
    del _L0_xattn_all

    def _L0_ffn_setup():
        import jax, jax.numpy as jnp
        import numpy as np
        B, T, D_IN, D_OUT = (8, 256, 512, 512)
        N_LORAS, RANK = (16, 32)
        SCALING = 1.0
        key = jax.random.key(seed)
        ks = jax.random.split(key, 8)
        std = 1.0 / D_IN ** 0.5
        x = jax.random.normal(ks[0], (B, T, D_IN), dtype=jnp.float32)
        idx = jax.random.randint(ks[1], (B,), 0, N_LORAS)
        gate = jax.nn.one_hot(idx, N_LORAS, dtype=jnp.float32)
        kernel = jax.random.normal(ks[2], (D_IN, D_OUT), dtype=jnp.float32) * std
        bias = jnp.zeros((D_OUT,), dtype=jnp.float32)
        lora_A = jax.random.normal(ks[3], (N_LORAS, RANK, D_IN), dtype=jnp.float32) * std
        lora_B = jax.random.normal(ks[4], (N_LORAS, D_OUT, RANK), dtype=jnp.float32) * 0.01
        lora_A_shared = jax.random.normal(ks[5], (RANK, D_IN), dtype=jnp.float32) * std
        lora_B_shared = jax.random.normal(ks[6], (D_OUT, RANK), dtype=jnp.float32) * 0.01
        return {'x': x, 'gate': gate, 'kernel': kernel, 'bias': bias, 'lora_A': lora_A, 'lora_B': lora_B, 'lora_A_shared': lora_A_shared, 'lora_B_shared': lora_B_shared}
    _L0_ffn_all = _L0_ffn_setup()
    _L0_ffn_in = {k: v for k, v in _L0_ffn_all.items() if k in ('gate', 'kernel', 'bias', 'lora_A', 'lora_B', 'lora_A_shared', 'lora_B_shared')}
    del _L0_ffn_all
    return {'x': x, 'ctx_4096': ctx_4096, 'pos_BxS2': pos_BxS2, 'mask_BxSxS2_ik0': mask_BxSxS2_ik0, 'L0_attn_w_q': _L0_attn_in['w_q'], 'L0_attn_w_k': _L0_attn_in['w_k'], 'L0_attn_w_v': _L0_attn_in['w_v'], 'L0_attn_w_o': _L0_attn_in['w_o'], 'L0_xattn_Wq': _L0_xattn_in['Wq'], 'L0_xattn_Wk': _L0_xattn_in['Wk'], 'L0_xattn_Wv': _L0_xattn_in['Wv'], 'L0_xattn_Wo': _L0_xattn_in['Wo'], 'L0_ffn_gate': _L0_ffn_in['gate'], 'L0_ffn_kernel': _L0_ffn_in['kernel'], 'L0_ffn_bias': _L0_ffn_in['bias'], 'L0_ffn_lora_A': _L0_ffn_in['lora_A'], 'L0_ffn_lora_B': _L0_ffn_in['lora_B'], 'L0_ffn_lora_A_shared': _L0_ffn_in['lora_A_shared'], 'L0_ffn_lora_B_shared': _L0_ffn_in['lora_B_shared']}

def reference(x, ctx_4096, pos_BxS2, mask_BxSxS2_ik0, L0_attn_w_q, L0_attn_w_k, L0_attn_w_v, L0_attn_w_o, L0_xattn_Wq, L0_xattn_Wk, L0_xattn_Wv, L0_xattn_Wo, L0_ffn_gate, L0_ffn_kernel, L0_ffn_bias, L0_ffn_lora_A, L0_ffn_lora_B, L0_ffn_lora_A_shared, L0_ffn_lora_B_shared):
    import jax
    import jax.numpy as jnp

    def _L0_attn_ref(x, w_q, w_k, w_v, w_o):
        import jax, jax.numpy as jnp
        import numpy as np
        HIDDEN = 512
        HEADS = 32
        D_K = HIDDEN // HEADS
        B, S, _ = x.shape

        def proj(w):
            y = jnp.einsum('bsd,ed->bse', x, w)
            return y.reshape(B, S, HEADS, D_K).transpose(0, 2, 1, 3)
        q, k, v = (proj(w_q), proj(w_k), proj(w_v))
        scores = jnp.einsum('bhqd,bhkd->bhqk', q, k) / jnp.sqrt(jnp.float32(D_K))
        attn = jax.nn.softmax(scores, axis=-1)
        out = jnp.einsum('bhqk,bhkd->bhqd', attn, v)
        out = out.transpose(0, 2, 1, 3).reshape(B, S, HIDDEN)
        return jnp.einsum('bse,oe->bso', out, w_o)

    def _L0_xattn_ref(query, key, value, position_ids, src_mask, Wq, Wk, Wv, Wo):
        import jax, jax.numpy as jnp
        import numpy as np
        B, S, E = (2, 256, 512)
        H, KVH, D = (32, 8, 128)
        GROUPS = H // KVH
        MAX_POS = 512
        ROPE_THETA = 10000.0

        def _rope_tables(max_pos, dim, theta):
            inv_freq = 1.0 / theta ** (jnp.arange(0, dim, 2, dtype=jnp.float32) / dim)
            t = jnp.arange(max_pos, dtype=jnp.float32)
            freqs = jnp.einsum('i,j->ij', t, inv_freq)
            emb = jnp.concatenate([freqs, freqs], axis=-1)
            return (jnp.cos(emb), jnp.sin(emb))

        def _rotate_half(x):
            x1, x2 = (x[..., :x.shape[-1] // 2], x[..., x.shape[-1] // 2:])
            return jnp.concatenate([-x2, x1], axis=-1)
        nb, q_len, _ = query.shape
        q = (query @ Wq).reshape(nb, q_len, H, D).transpose(0, 2, 1, 3)
        k = (key @ Wk).reshape(nb, q_len, KVH, D).transpose(0, 2, 1, 3)
        v = (value @ Wv).reshape(nb, q_len, KVH, D).transpose(0, 2, 1, 3)
        cos_t, sin_t = _rope_tables(MAX_POS, D, ROPE_THETA)
        cos = cos_t[position_ids][:, None]
        sin = sin_t[position_ids][:, None]
        q = q * cos + _rotate_half(q) * sin
        k = k * cos + _rotate_half(k) * sin
        k = jnp.repeat(k, GROUPS, axis=1)
        v = jnp.repeat(v, GROUPS, axis=1)
        scores = jnp.einsum('bhqd,bhkd->bhqk', q, k) / jnp.sqrt(jnp.float32(D))
        mask = src_mask[:, None]
        scores = jnp.where(mask == 0, jnp.float32(-1000000000.0), scores)
        attn = jax.nn.softmax(scores, axis=-1)
        x = jnp.einsum('bhqk,bhkd->bhqd', attn, v)
        x = x.transpose(0, 2, 1, 3).reshape(nb, q_len, H * D)
        return x @ Wo

    def _L0_ffn_ref(x, gate, kernel, bias, lora_A, lora_B, lora_A_shared, lora_B_shared):
        import jax, jax.numpy as jnp
        import numpy as np
        B, T, D_IN, D_OUT = (8, 256, 512, 512)
        N_LORAS, RANK = (16, 32)
        SCALING = 1.0
        base_out = jnp.matmul(x, kernel) + bias
        b = gate.shape[0]
        x_flat = x.reshape(b, -1, x.shape[-1])
        A_eff = jnp.einsum('bn,nri->bri', gate, lora_A)
        B_eff = jnp.einsum('bn,nor->bor', gate, lora_B)
        Ax = jnp.einsum('bri,bti->btr', A_eff, x_flat)
        delta_flat = jnp.einsum('bor,btr->bto', B_eff, Ax)
        Ax_s = jnp.einsum('ri,bti->btr', lora_A_shared, x_flat)
        delta_flat = delta_flat + jnp.einsum('or,btr->bto', lora_B_shared, Ax_s)
        delta = delta_flat.reshape(x.shape[:-1] + (kernel.shape[-1],))
        return base_out + (SCALING * delta).astype(base_out.dtype)
    x = x + _L0_attn_ref(_layernorm(x, axis=-1), L0_attn_w_q, L0_attn_w_k, L0_attn_w_v, L0_attn_w_o)
    x = x + _L0_xattn_ref(_layernorm(x, axis=-1), ctx_4096, ctx_4096, pos_BxS2, mask_BxSxS2_ik0, L0_xattn_Wq, L0_xattn_Wk, L0_xattn_Wv, L0_xattn_Wo)
    x = x + _L0_ffn_ref(_layernorm(x, axis=-1), L0_ffn_gate, L0_ffn_kernel, L0_ffn_bias, L0_ffn_lora_A, L0_ffn_lora_B, L0_ffn_lora_A_shared, L0_ffn_lora_B_shared)
    return x

_drawn_inputs = setup_inputs


def setup_inputs(seed=0):
    import zlib

    import numpy as np

    out = dict(_drawn_inputs(seed))
    spreads = {'L0_ffn_bias': (0.0, 0.1)}
    factors = {'L0_attn_w_q': 5.87, 'L0_attn_w_k': 5.421}
    for name, (base, spread) in spreads.items():
        noise = np.random.default_rng([zlib.crc32(name.encode()), seed]).standard_normal(out[name].shape)
        drawn = base * np.exp(spread * noise) if base else spread * noise
        out[name] = jnp.asarray(drawn.astype(out[name].dtype))
    for name, factor in factors.items():
        out[name] = (out[name] * factor).astype(out[name].dtype)
    return out
```

```python
import numpy as np
import concourse.bass as bass
from concourse import mybir

F32 = mybir.dt.float32
F32R = mybir.dt.float32r
I32 = mybir.dt.int32
ALU = mybir.AluOpType
ACT = mybir.ActivationFunctionType
AX = mybir.AxisListType

P = 128
BATCH, SEQ, HIDDEN = 32, 64, 512
TOKENS = BATCH * SEQ
TILES = TOKENS // P
BLOCK = 512
NB = TOKENS // BLOCK
TPB = BLOCK // P
KC = HIDDEN // P
EPS = 1e-5
H1, D1 = 32, 16
HPG1 = P // D1
G1 = H1 // HPG1
VPITCH = P + D1
VROW = HPG1 * VPITCH
H2, KVH, D2 = 32, 8, 128
HPG2 = H2 // KVH
HALF = D2 // 2
MAX_POS = 512
MASKED = -1e9 * float(np.sqrt(np.float32(D2)))
OPEN = 3.0e38
LB, NLORA, RANK = 8, 16, 32
NPC = P // RANK
NCH = NLORA // NPC


def need(engine, semaphore, value):
    if not isinstance(value, int) or value > 0:
        engine.wait_ge(semaphore, value)


def exists(index, count):
    return not isinstance(index, int) or 0 <= index < count


def ds(start, size):
    return slice(start, start + size) if isinstance(start, int) else bass.ds(start, size)


def product3(nc, out, chunks):
    last = len(chunks) - 1
    for c, (lh, ll, rh, rl) in enumerate(chunks):
        nc.tensor.matmul(out, lh, rh, start=(c == 0), stop=False)
        nc.tensor.matmul(out, lh, rl, start=False, stop=False)
        mm = nc.tensor.matmul(out, ll, rh, start=False, stop=(c == last))
    return mm


def walk(engine, groups, body):
    def row(g):
        body(g, 0)
        with engine.Fori(1, NB - 1) as b:
            body(g, b)
        body(g, NB - 1)
    for b in range(NB):
        body(0, b)
    with engine.Fori(1, groups - 1) as g:
        row(g)
    row(groups - 1)


class Memory:

    def __init__(self, nc, stack, prefix):
        self.nc, self.stack, self.prefix = nc, stack, prefix

    def sb(self, name, shape, dt=F32):
        return self.stack.enter_context(self.nc.sbuf_tensor(self.prefix + name, shape, dt))

    def ps(self, name, shape=(P, 512)):
        return self.stack.enter_context(self.nc.psum_tensor(self.prefix + name, list(shape), F32))

    def sem(self, name):
        return self.stack.enter_context(self.nc.semaphore(self.prefix + name))


def statistics_memory(m):
    return dict(stats=m.sb("stats", [P, TILES, 6]), mv=m.sb("mv", [P, TILES, 2]), sd=m.sb("sd", [P, TILES]),
                rstd=m.sb("rstd", [P, TILES]), stat=m.sem("stat"), var=m.sem("var"), root=m.sem("root"),
                norm=m.sem("norm"))


def statistics_vector(nc, dve, x, L, arrived=None):
    for t in range(TILES):
        if arrived is not None and t % TPB == 0:
            dve.wait_ge(arrived[t // TPB], 16)
        nc.vector.bn_stats(L["stats"][:, t, :], x[:, t, :]).then_inc(L["stat"], 1)
    for t in range(TILES):
        dve.wait_ge(L["stat"], t + 1)
        nc.vector.bn_aggr(L["mv"][:, t, :], L["stats"][:, t, :]).then_inc(L["var"], 1)
    dve.wait_ge(L["var"], TILES)
    nc.vector.tensor_scalar(L["sd"][:, :], L["mv"][:, :, 1], EPS, None, ALU.add).then_inc(L["var"], 1)
    dve.wait_ge(L["root"], 1)
    nc.vector.reciprocal(L["rstd"][:, :], L["sd"][:, :]).then_inc(L["norm"], 1)
    dve.wait_ge(L["norm"], 1)


def statistics_scalar(nc, act, L):
    act.wait_ge(L["var"], TILES + 1)
    nc.scalar.activation(L["sd"][:, :], L["sd"][:, :], ACT.Sqrt).then_inc(L["root"], 1)


def normalise(nc, out, x, L, t):
    return nc.vector.tensor_scalar(out, x[:, ds(t, 1), :].squeeze(1) if not isinstance(t, int) else x[:, t, :],
                                   L["mv"][:, ds(t, 1), 0], L["rstd"][:, ds(t, 1)], ALU.subtract, ALU.mult)


def transpose_chunks(nc, out, src, ident):
    for c in range(KC):
        tr = nc.tensor.transpose(out[:, c * P:(c + 1) * P], src[:, c * P:(c + 1) * P], ident[:, :])
    return tr


def norm_and_values(nc, stack_type, x, xt_hi, xt_lo, v1, ident, x_dram, wv_dram, ident_dram):
    with stack_type() as stack:
        m = Memory(nc, stack, "p1_")
        L = statistics_memory(m)
        wv_raw = m.sb("wv_raw", [P, KC, HIDDEN])
        wv_hi, wv_lo = (m.sb(n, [P, KC, HIDDEN], F32R) for n in ("wv_hi", "wv_lo"))
        xn = [m.sb(f"xn{u}", [P, HIDDEN]) for u in range(2)]
        t_hi = [m.sb(f"t_hi{u}", [P, KC, P], F32R) for u in range(2)]
        t_lo = [m.sb(f"t_lo{u}", [P, KC, P], F32R) for u in range(2)]
        ps_t = [m.ps(f"ps_t{u}") for u in range(2)]
        ps_v = [m.ps(f"ps_v{u}") for u in range(2)]
        x_in = [m.sem(f"x_in{b}") for b in range(NB)]
        w_in, id_in, w_hi, w_ready = m.sem("w_in"), m.sem("id_in"), m.sem("w_hi"), m.sem("w_ready")
        xn_ready, transposed = m.sem("xn_ready"), m.sem("transposed")
        all_hi, tile_lo, all_lo = m.sem("all_hi"), m.sem("tile_lo"), m.sem("all_lo")
        v_done, v_copied = m.sem("v_done"), m.sem("v_copied")

        def tiles(engine, body):
            for n in range(4):
                body(n, n % 2)
            with engine.Fori(2, TILES // 2 - 1) as i:
                body(i * 2, 0)
                body(i * 2 + 1, 1)
            body(TILES - 2, 0)
            body(TILES - 1, 1)

        block = stack.enter_context(nc.Block())

        @block.sync
        def _(sp):
            for b in range(NB):
                sp.dma_start(x[:, b * TPB:(b + 1) * TPB, :], x_dram[:, b * TPB:(b + 1) * TPB, :]).then_inc(x_in[b], 16)
            sp.dma_start(ident[:, :], ident_dram).then_inc(id_in, 16)
            sp.dma_start(wv_raw[:, :, :], wv_dram).then_inc(w_in, 16)

        @block.scalar
        def _(act):
            act.wait_ge(w_in, 16)
            nc.scalar.activation(wv_hi[:, :, :], wv_raw[:, :, :], ACT.Copy).then_inc(w_hi, 1)
            statistics_scalar(nc, act, L)

            def copy_values(n):
                need(act, v_done, n + 1)
                nc.scalar.activation(v1[:, ds(n, 1), :], ps_v[slot_of[0]][:, :].unsqueeze(1), ACT.Copy).then_inc(v_copied, 1)

            slot_of = [0]

            def body(n, u):
                need(act, transposed, n + 1)
                need(act, v_done, n - 1)
                nc.scalar.activation(t_hi[u][:, :, :], ps_t[u][:, :].rearrange("p (c n) -> p c n", c=KC), ACT.Copy)
                nc.scalar.activation(xt_hi[:, :, ds(n * P, P)], ps_t[u][:, :].rearrange("p (c n) -> p c n", c=KC), ACT.Copy).then_inc(all_hi, 1)
                slot_of[0] = 1 - u
                if exists(n - 1, TILES):
                    copy_values(n - 1)
            tiles(act, body)
            slot_of[0] = 1
            copy_values(TILES - 1)

        @block.vector
        def _(dve):
            statistics_vector(nc, dve, x, L, x_in)

            def norm(n, u):
                need(dve, transposed, n - 1)
                normalise(nc, xn[u][:, :], x, L, n).then_inc(xn_ready, 1)

            norm(0, 0)
            dve.wait_ge(w_hi, 1)
            nc.vector.tensor_tensor(wv_lo[:, :, :], wv_raw[:, :, :], wv_hi[:, :, :], ALU.subtract).then_inc(w_ready, 1)

            def body(n, u):
                if exists(n + 1, TILES):
                    norm(n + 1, 1 - u)
                need(dve, all_hi, n + 1)
                need(dve, all_lo, n - 1)
                nc.vector.tensor_tensor(t_lo[u][:, :, :], ps_t[u][:, :].rearrange("p (c n) -> p c n", c=KC),
                                        t_hi[u][:, :, :], ALU.subtract).then_inc(tile_lo, 1)
            tiles(dve, body)

        @block.gpsimd
        def _(pool):
            def body(n, u):
                need(pool, tile_lo, n + 1)
                nc.gpsimd.tensor_copy(xt_lo[:, :, ds(n * P, P)], t_lo[u][:, :, :]).then_inc(all_lo, 1)
            tiles(pool, body)

        @block.tensor
        def _(pe):
            pe.wait_ge(id_in, 16)

            def values(n, u):
                need(pe, tile_lo, n + 1)
                need(pe, v_copied, n - 1)
                product3(nc, ps_v[u][:, :], [(t_hi[u][:, c, :], t_lo[u][:, c, :], wv_hi[:, c, :], wv_lo[:, c, :])
                                             for c in range(KC)]).then_inc(v_done, 1)

            def body(n, u):
                need(pe, xn_ready, n + 1)
                need(pe, tile_lo, n - 1)
                need(pe, all_hi, n - 1)
                transpose_chunks(nc, ps_t[u], xn[u], ident).then_inc(transposed, 1)
                if isinstance(n, int) and n == 1:
                    pe.wait_ge(w_ready, 1)
                if exists(n - 1, TILES):
                    values(n - 1, 1 - u)
            tiles(pe, body)
            values(TILES - 1, 1)


def self_attention(nc, stack_type, x, xt_hi, xt_lo, v1, ident, wq_dram, wk_dram, wo_dram, heads_dram):
    with stack_type() as stack:
        m = Memory(nc, stack, "p2_")
        SCALE = 1.0 / float(np.sqrt(np.float32(D1)))
        ITS = G1 * NB
        SCORES, EXPS, NORMS = 3, 2, 1

        def ahead(it, j, k):
            return (it, j + k) if j + k < HPG1 else (it + 1, j + k - HPG1)
        raw = {w: m.sb(f"raw_{w}", [P, KC, P]) for w in "qk"}
        w_hi = {w: m.sb(f"w{w}_hi", [P, KC, P], F32R) for w in "qk"}
        w_lo = {w: m.sb(f"w{w}_lo", [P, KC, P], F32R) for w in "qk"}
        wo_raw = m.sb("wo_raw", [P, HIDDEN])
        wo_hi, wo_lo = m.sb("wo_hi", [P, HIDDEN], F32R), m.sb("wo_lo", [P, HIDDEN], F32R)
        heads = m.sb("heads", [P, HPG1])
        q_t, k_t = m.sb("q_t", [P, BLOCK]), m.sb("k_t", [P, BLOCK])
        q_head = m.sb("q_head", [P, HPG1, BLOCK])
        v_head = m.sb("v_head", [P, TPB, VROW])
        s = [m.sb(f"s{i}", [P, TPB, SEQ]) for i in range(2)]
        p = [m.sb(f"p{i}", [P, TPB, SEQ]) for i in range(2)]
        pd = [m.sb(f"pd{i}", [P, TPB, P]) for i in range(2)]
        pt = [m.sb(f"pt{i}", [P, BLOCK]) for i in range(2)]
        mx = [m.sb(f"mx{i}", [P, TPB]) for i in range(2)]
        total = [m.sb(f"total{i}", [P, TPB]) for i in range(2)]
        inv = [m.sb(f"inv{i}", [P, TPB]) for i in range(2)]
        o_hi, o_lo = m.sb("o_hi", [P, BLOCK], F32R), m.sb("o_lo", [P, BLOCK], F32R)
        ps_qk, ps_o = m.ps("ps_qk"), m.ps("ps_o")
        ps_s = [m.ps(f"ps_s{i}") for i in range(2)]
        ps_p = [m.ps(f"ps_p{i}") for i in range(2)]
        ps_y = [m.ps(f"ps_y{i}") for i in range(2)]
        raw_in = {w: m.sem(f"raw_in_{w}") for w in "qko"}
        part_hi = {w: m.sem(f"part_hi_{w}") for w in "qko"}
        ready = {w: m.sem(f"ready_{w}") for w in "qko"}
        heads_in, zeroed = m.sem("heads_in"), m.sem("zeroed")
        done = {"q": m.sem("q_done"), "k": m.sem("k_done")}
        q_copied, k_copied, expanded = m.sem("q_copied"), m.sem("k_copied"), m.sem("expanded")
        s_done, s_max, s_shifted = m.sem("s_done"), m.sem("s_max"), m.sem("s_shifted")
        p_exp, p_inv, p_norm, p_turned, pt_copied = (m.sem(n) for n in ("p_exp", "p_inv", "p_norm", "p_turned", "pt_copied"))
        v_ready, pv_done, out_hi, out_lo, y_done, y_added = (m.sem(n) for n in ("v_ready", "pv_done", "out_hi", "out_lo", "y_done", "y_added"))
        vh = v_head[:, :, :].rearrange("p t (j w) -> p t j w", w=VPITCH)[:, :, :, 0:D1]

        block = stack.enter_context(nc.Block())

        @block.sync
        def _(sp):
            sp.dma_start(heads[:, :], heads_dram).then_inc(heads_in, 16)

            def load(g):
                need(sp, ready["q"], g)
                sp.dma_start(raw["q"][:, :, :], wq_dram[:, :, ds(g * P, P)]).then_inc(raw_in["q"], 16)
                need(sp, ready["k"], g)
                sp.dma_start(raw["k"][:, :, :], wk_dram[:, :, ds(g * P, P)]).then_inc(raw_in["k"], 16)
                need(sp, ready["o"], g)
                sp.dma_start(wo_raw[:, :], wo_dram[ds(g * P, P), :]).then_inc(raw_in["o"], 16)
            load(0)
            with sp.Fori(1, G1) as g:
                load(g)

        def split_hi(act, w, g, after, count):
            need(act, raw_in[w], (g + 1) * 16)
            need(act, after, count)
            dst, src = (wo_hi[:, :], wo_raw[:, :]) if w == "o" else (w_hi[w][:, :, :], raw[w][:, :, :])
            nc.scalar.activation(dst, src, ACT.Copy).then_inc(part_hi[w], 1)

        def split_lo(dve, w, g):
            need(dve, part_hi[w], g + 1)
            if w == "o":
                sub = nc.vector.tensor_tensor(wo_lo[:, :], wo_raw[:, :], wo_hi[:, :], ALU.subtract)
            else:
                sub = nc.vector.tensor_tensor(w_lo[w][:, :, :], raw[w][:, :, :], w_hi[w][:, :, :], ALU.subtract)
            sub.then_inc(ready[w], 1)

        def next_group(g, b):
            return g + 1 if isinstance(b, int) and b == NB - 1 else g

        @block.tensor
        def _(pe):
            def project(w, g, it, nb):
                need(pe, ready[w], g + 1)
                if w == "q":
                    need(pe, k_copied, it)
                else:
                    need(pe, q_copied, it + 1)
                product3(nc, ps_qk[:, :], [(w_hi[w][:, c, :], w_lo[w][:, c, :], xt_hi[:, c, ds(nb * BLOCK, BLOCK)],
                                            xt_lo[:, c, ds(nb * BLOCK, BLOCK)]) for c in range(KC)]).then_inc(done[w], 1)

            def scores(it, j):
                u = it * HPG1 + j
                need(pe, expanded, u + 1)
                need(pe, k_copied, it + 1)
                need(pe, s_shifted, u - 1)
                for t in range(TPB):
                    mm = nc.tensor.matmul(ps_s[j % 2][:, t * P:(t + 1) * P], q_head[:, j, t * P:(t + 1) * P],
                                          k_t[:, t * P:(t + 1) * P], start=True, stop=True)
                mm.then_inc(s_done, 1)

            def turn(it, j):
                u = it * HPG1 + j
                need(pe, p_norm, u + 1)
                need(pe, pt_copied, u - 1)
                for t in range(TPB):
                    tr = nc.tensor.transpose(ps_p[j % 2][:, t * P:(t + 1) * P], pd[j % 2][:, t, :], ident[:, :])
                tr.then_inc(p_turned, 1)

            def mix(it, j):
                u = it * HPG1 + j
                need(pe, pt_copied, u + 1)
                if j == 0:
                    need(pe, v_ready, it + 1)
                    need(pe, out_lo, it)
                for t in range(TPB):
                    mm = nc.tensor.matmul(ps_o[:, t * P:(t + 1) * P], v_head[:, t, j * P:(j + 1) * P],
                                          pt[j % 2][:, t * P:(t + 1) * P], start=(j == 0 and t == 0),
                                          stop=(j == HPG1 - 1), skip_group_check=True)
                mm.then_inc(pv_done, 1)

            def output(g, it, tiles):
                need(pe, out_lo, it + 1)
                need(pe, ready["o"], g + 1)
                for t in tiles:
                    need(pe, y_added, it * TPB + t - 1)
                    product3(nc, ps_y[t % 2][:, :], [(o_hi[:, t * P:(t + 1) * P], o_lo[:, t * P:(t + 1) * P],
                                                      wo_hi[:, :], wo_lo[:, :])]).then_inc(y_done, 1)

            def body(g, b):
                it = g * NB + b
                nb = 0 if isinstance(b, int) and b == NB - 1 else b + 1
                for j in range(HPG1):
                    if exists(ahead(it, j, SCORES)[0], ITS):
                        scores(*ahead(it, j, SCORES))
                    if exists(it + 1, ITS) and j == 1:
                        project("q", next_group(g, b), it + 1, nb)
                    if exists(it + 1, ITS) and j == 4:
                        project("k", next_group(g, b), it + 1, nb)
                    turn(it, j)
                    if j in (3, 5) and exists(it - 1, ITS):
                        output(g - 1 if isinstance(b, int) and b == 0 else g, it - 1, (j - 3, j - 2))
                    if j > 0:
                        mix(it, j - 1)
                    elif exists(it - 1, ITS):
                        mix(it - 1, HPG1 - 1)

            project("q", 0, 0, 0)
            project("k", 0, 0, 0)
            for j in range(SCORES):
                scores(0, j)
            walk(pe, G1, body)
            mix(ITS - 1, HPG1 - 1)
            output(G1 - 1, ITS - 1, range(TPB))

        @block.scalar
        def _(act):
            def copy(w, it):
                need(act, done[w], it + 1)
                if w == "q":
                    need(act, expanded, it * HPG1)
                    nc.scalar.activation(q_t[:, :], ps_qk[:, :], ACT.Copy).then_inc(q_copied, 1)
                else:
                    need(act, s_done, it * HPG1)
                    nc.scalar.activation(k_t[:, :], ps_qk[:, :], ACT.Copy).then_inc(k_copied, 1)

            def expand(it, j):
                need(act, q_copied, it + 1)
                need(act, s_done, it * HPG1 + j + 1 - HPG1)
                nc.scalar.activation(q_head[:, j, :], q_t[:, :], ACT.Copy, scale=heads[:, j:j + 1]).then_inc(expanded, 1)

            def exponentials(it, j):
                u = it * HPG1 + j
                need(act, s_shifted, u + 1)
                need(act, p_norm, u - 1)
                for t in range(TPB):
                    e = nc.scalar.activation(p[j % 2][:, t, :], s[j % 2][:, t, :], ACT.Exp, scale=SCALE,
                                             accum_out=total[j % 2][:, t:t + 1])
                e.then_inc(p_exp, 1)

            def copy_turned(it, j):
                u = it * HPG1 + j
                need(act, p_turned, u + 1)
                need(act, pv_done, u - 1)
                nc.scalar.activation(pt[j % 2][:, :], ps_p[j % 2][:, :], ACT.Copy).then_inc(pt_copied, 1)

            def outputs_hi(it):
                need(act, pv_done, (it + 1) * HPG1)
                need(act, y_done, it * TPB)
                nc.scalar.activation(o_hi[:, :], ps_o[:, :], ACT.Copy).then_inc(out_hi, 1)

            def body(g, b):
                it = g * NB + b
                last_block, first_block = (isinstance(b, int) and b == NB - 1), (isinstance(b, int) and b == 0)
                for j in range(HPG1):
                    if exists(it + 1, ITS) and last_block and j == 0:
                        split_hi(act, "q", g + 1, done["q"], it + 1)
                    if exists(it + 1, ITS) and last_block and j == 2:
                        split_hi(act, "k", g + 1, done["k"], it + 1)
                    if first_block and exists(it - 1, ITS) and j == 6:
                        split_hi(act, "o", g, y_done, it * TPB)
                    if j == 1 and exists(it - 1, ITS):
                        outputs_hi(it - 1)
                    if j == 2 and exists(it + 1, ITS):
                        copy("q", it + 1)
                    copy_turned(it, j)
                    if j == 4 and exists(it + 1, ITS):
                        copy("k", it + 1)
                    if exists(ahead(it, j, EXPS)[0], ITS):
                        exponentials(*ahead(it, j, EXPS))
                    if j < 2:
                        expand(it, HPG1 - 2 + j)
                    elif exists(it + 1, ITS):
                        expand(it + 1, j - 2)

            split_hi(act, "q", 0, done["q"], 0)
            split_hi(act, "k", 0, done["k"], 0)
            split_hi(act, "o", 0, y_done, 0)
            copy("q", 0)
            copy("k", 0)
            act.wait_ge(heads_in, 16)
            for j in range(HPG1 - 2):
                expand(0, j)
            for j in range(EXPS):
                exponentials(0, j)
            walk(act, G1, body)
            outputs_hi(ITS - 1)

        @block.vector
        def _(dve):
            def shift(it, j):
                u = it * HPG1 + j
                sc = ps_s[j % 2][:, :].rearrange("p (t k) -> p t k", t=TPB)
                need(dve, s_done, u + 1)
                for r in range(2):
                    rows = slice(r * SEQ, (r + 1) * SEQ)
                    red = nc.vector.tensor_reduce(mx[j % 2][rows, :], sc[rows, :, rows], AX.X, ALU.max)
                red.then_inc(s_max, 1)
                need(dve, s_max, u + 1)
                need(dve, p_exp, u - 1)
                for r in range(2):
                    rows = slice(r * SEQ, (r + 1) * SEQ)
                    sub = nc.vector.tensor_tensor(s[j % 2][rows, :, :], sc[rows, :, rows],
                                                  mx[j % 2][rows, :].unsqueeze(2).broadcast_to([SEQ, TPB, SEQ]), ALU.subtract)
                sub.then_inc(s_shifted, 1)

            def invert(it, j):
                need(dve, p_exp, it * HPG1 + j + 1)
                nc.vector.reciprocal(inv[j % 2][:, :], total[j % 2][:, :]).then_inc(p_inv, 1)

            def outputs_lo(it):
                need(dve, out_hi, it + 1)
                nc.vector.tensor_tensor(o_lo[:, :], ps_o[:, :], o_hi[:, :], ALU.subtract).then_inc(out_lo, 1)

            def pad_values(g, b, it):
                need(dve, pv_done, it * HPG1)
                nc.vector.tensor_copy(vh, v1[:, ds(b * TPB, TPB), ds(g * P, P)].rearrange("p t (j w) -> p t j w", w=D1)).then_inc(v_ready, 1)

            def add(b, it, tiles):
                for t in tiles:
                    need(dve, y_done, it * TPB + t + 1)
                    need(dve, y_added, it * TPB + t)
                    xs = x[:, ds(b * TPB + t, 1), :]
                    nc.vector.tensor_tensor(xs, ps_y[t % 2][:, :].unsqueeze(1), xs, ALU.add).then_inc(y_added, 1)

            def body(g, b):
                it = g * NB + b
                last_block, first_block = (isinstance(b, int) and b == NB - 1), (isinstance(b, int) and b == 0)
                for j in range(HPG1):
                    if exists(it + 1, ITS) and last_block and j == 0:
                        split_lo(dve, "q", g + 1)
                    if exists(it + 1, ITS) and last_block and j == 2:
                        split_lo(dve, "k", g + 1)
                    if exists(ahead(it, j, NORMS)[0], ITS):
                        invert(*ahead(it, j, NORMS))
                    if j == 1:
                        if exists(it - 1, ITS):
                            outputs_lo(it - 1)
                        pad_values(g, b, it)
                    if exists(ahead(it, j, SCORES)[0], ITS):
                        shift(*ahead(it, j, SCORES))
                    if j in (4, 6) and exists(it - 1, ITS):
                        add(NB - 1 if first_block else b - 1, it - 1, (j - 4, j - 3))
                    if first_block and exists(it - 1, ITS) and j == 6:
                        split_lo(dve, "o", g)

            nc.vector.memset(v_head[:, :, :], 0.0).then_inc(zeroed, 1)
            for i in range(2):
                nc.vector.memset(pd[i][:, :, :], 0.0).then_inc(zeroed, 1)
            for w in "qko":
                split_lo(dve, w, 0)
            dve.wait_ge(zeroed, 3)
            for j in range(SCORES):
                shift(0, j)
            invert(0, 0)
            walk(dve, G1, body)
            outputs_lo(ITS - 1)
            add(NB - 1, ITS - 1, range(TPB))

        @block.gpsimd
        def _(pool):
            def normalise_p(it, j):
                u = it * HPG1 + j
                need(pool, p_inv, u + 1)
                need(pool, p_turned, u - 1)
                for r in range(2):
                    rows = slice(r * SEQ, (r + 1) * SEQ)
                    mul = nc.gpsimd.tensor_tensor(pd[j % 2][rows, :, rows], p[j % 2][rows, :, :],
                                                  inv[j % 2][rows, :].unsqueeze(2).broadcast_to([SEQ, TPB, SEQ]), ALU.mult)
                mul.then_inc(p_norm, 1)

            def body(g, b):
                it = g * NB + b
                for j in range(HPG1):
                    if exists(ahead(it, j, NORMS)[0], ITS):
                        normalise_p(*ahead(it, j, NORMS))

            pool.wait_ge(zeroed, 3)
            normalise_p(0, 0)
            walk(pool, G1, body)


def rotate_terms(nc, ps, cos, sin, a, b):
    nc.vector.tensor_tensor(a[:, :], ps[:, :], cos, ALU.mult)
    nc.vector.tensor_tensor(b[0:HALF, :], ps[HALF:D2, :], sin[HALF:D2], ALU.mult)
    return nc.vector.tensor_tensor(b[HALF:D2, :], ps[0:HALF, :], sin[0:HALF], ALU.mult)


def keys_and_values(nc, stack_type, cos_t, sin_t, ident, pos_dram, table_dram, ctx_dram, wk_dram, wv_dram, k_scr, v_scr):
    with stack_type() as stack:
        m = Memory(nc, stack, "p3_")
        NKV = KVH * D2
        UPB = 2 * KVH
        pos = m.sb("pos", [P, TILES], mybir.dt.uint32)
        rows = m.sb("rows", [P, TILES, 2 * D2])
        raw = {w: m.sb(f"raw_{w}", [P, KC, NKV]) for w in "kv"}
        w_hi = {w: m.sb(f"w{w}_hi", [P, KC, NKV], F32R) for w in "kv"}
        w_lo = {w: m.sb(f"w{w}_lo", [P, KC, NKV], F32R) for w in "kv"}
        c_raw = m.sb("c_raw", [P, KC, BLOCK])
        c_hi, c_lo = m.sb("c_hi", [P, KC, BLOCK], F32R), m.sb("c_lo", [P, KC, BLOCK], F32R)
        ra, rb = m.sb("ra", [P, BLOCK]), m.sb("rb", [P, BLOCK])
        k_out = [m.sb(f"k_out{i}", [P, BLOCK]) for i in range(2)]
        v_out = [m.sb(f"v_out{i}", [P, BLOCK]) for i in range(2)]
        ps_r = [m.ps(f"ps_r{i}") for i in range(2)]
        ps_k = [m.ps(f"ps_k{i}") for i in range(2)]
        ps_v = [m.ps(f"ps_v{i}") for i in range(2)]
        pos_in, row_in, row_turned, row_copied = (m.sem(n) for n in ("pos_in", "row_in", "row_turned", "row_copied"))
        raw_in = {w: m.sem(f"raw_in_{w}") for w in "kv"}
        part_hi, ready = {w: m.sem(f"part_hi_{w}") for w in "kv"}, {w: m.sem(f"ready_{w}") for w in "kv"}
        c_in, c_part, c_ready = m.sem("c_in"), m.sem("c_part"), m.sem("c_ready")
        k_done, v_done, k_terms, k_added, v_copied = (m.sem(n) for n in ("k_done", "v_done", "k_terms", "k_added", "v_copied"))
        k_stored, v_stored = [m.sem(f"k_stored{i}") for i in range(2)], [m.sem(f"v_stored{i}") for i in range(2)]
        block = stack.enter_context(nc.Block())

        def blocks(engine, body):
            body(0)
            with engine.Fori(1, NB) as b:
                body(b)

        @block.sync
        def _(sp):
            sp.dma_start(pos[:, :], pos_dram).then_inc(pos_in, 16)
            sp.dma_start(raw["k"][:, :, :], wk_dram).then_inc(raw_in["k"], 16)
            sp.dma_start(c_raw[:, :, :], ctx_dram[:, :, 0:BLOCK]).then_inc(c_in, 16)
            sp.dma_start(raw["v"][:, :, :], wv_dram).then_inc(raw_in["v"], 16)

            def body(b):
                if not isinstance(b, int):
                    need(sp, c_ready, b * KC)
                    sp.dma_start(c_raw[:, :, :], ctx_dram[:, :, ds(b * BLOCK, BLOCK)]).then_inc(c_in, 16)
                for i in range(KVH):
                    n = b * KVH + i
                    need(sp, k_added, n + 1)
                    sp.dma_start(k_scr[i, ds(b, 1), :, :].squeeze(0) if not isinstance(b, int) else k_scr[i, b, :, :],
                                 k_out[i % 2][:, :]).then_inc(k_stored[i % 2], 16)
                    need(sp, v_copied, n + 1)
                    t, h = i // 2, i % 2
                    g0 = h * (KVH // 2)
                    dst = v_scr[g0:g0 + KVH // 2, ds(b, 1), :, t, :].squeeze(1) if not isinstance(b, int) else v_scr[g0:g0 + KVH // 2, b, :, t, :]
                    sp.dma_start(dst.rearrange("g p d -> p g d"),
                                 v_out[i % 2][:, :].rearrange("p (g d) -> p g d", d=D2)).then_inc(v_stored[i % 2], 16)
            blocks(sp, body)
            for i in range(2):
                sp.wait_ge(k_stored[i], 16 * NB * KVH // 2)
                sp.wait_ge(v_stored[i], 16 * NB * KVH // 2)

        @block.gpsimd
        def _(pool):
            pool.wait_ge(pos_in, 16)
            for t in range(TILES):
                pool.indirect_dma_start(rows[:, t, :], None, table_dram, bass.IndirectOffsetOnAxis(ap=pos[:, t:t + 1], axis=0)).then_inc(row_in, 16)

            def body(b):
                for i in range(KVH):
                    n = b * KVH + i
                    need(pool, k_terms, n + 1)
                    need(pool, k_stored[i % 2], (b * (KVH // 2) + i // 2) * 16)
                    nc.gpsimd.tensor_tensor(k_out[i % 2][:, :], ra[:, :], rb[:, :], ALU.add).then_inc(k_added, 1)
            blocks(pool, body)

        @block.scalar
        def _(act):
            for w in "kv":
                act.wait_ge(raw_in[w], 16)
                nc.scalar.activation(w_hi[w][:, :, :], raw[w][:, :, :], ACT.Copy).then_inc(part_hi[w], 1)
                if w == "k":
                    for n in range(2 * NB):
                        act.wait_ge(row_turned, n + 1)
                        dst = (cos_t, sin_t)[n % 2]
                        nc.scalar.activation(dst[:, (n // 2) * BLOCK:(n // 2 + 1) * BLOCK], ps_r[n % 2][:, :], ACT.Copy).then_inc(row_copied, 1)

            def body(b):
                need(act, c_in, (b + 1) * 16)
                need(act, k_done, b * KVH)
                need(act, v_done, b * KVH)
                for c in range(KC):
                    nc.scalar.activation(c_hi[:, c, :], c_raw[:, c, :], ACT.Copy).then_inc(c_part, 1)
                for i in range(KVH):
                    n = b * KVH + i
                    need(act, v_done, n + 1)
                    need(act, v_stored[i % 2], (b * (KVH // 2) + i // 2) * 16)
                    nc.scalar.activation(v_out[i % 2][:, :], ps_v[i % 2][:, :], ACT.Copy).then_inc(v_copied, 1)
            blocks(act, body)

        @block.vector
        def _(dve):
            for w in "kv":
                dve.wait_ge(part_hi[w], 1)
                nc.vector.tensor_tensor(w_lo[w][:, :, :], raw[w][:, :, :], w_hi[w][:, :, :], ALU.subtract).then_inc(ready[w], 1)
            dve.wait_ge(row_copied, 2 * NB)

            def body(b):
                for c in range(KC):
                    need(dve, c_part, b * KC + c + 1)
                    nc.vector.tensor_tensor(c_lo[:, c, :], c_raw[:, c, :], c_hi[:, c, :], ALU.subtract).then_inc(c_ready, 1)
                for i in range(KVH):
                    n = b * KVH + i
                    need(dve, k_done, n + 1)
                    need(dve, k_added, n)
                    rotate_terms(nc, ps_k[i % 2], cos_t[:, ds(b * BLOCK, BLOCK)], sin_t[:, ds(b * BLOCK, BLOCK)], ra, rb).then_inc(k_terms, 1)
            blocks(dve, body)

        @block.tensor
        def _(pe):
            for n in range(2 * NB):
                blk, part = n // 2, n % 2
                pe.wait_ge(row_in, 16 * TILES)
                need(pe, row_copied, n - 1)
                for t in range(TPB):
                    tr = nc.tensor.transpose(ps_r[part][:, t * P:(t + 1) * P], rows[:, blk * TPB + t, part * D2:(part + 1) * D2], ident[:, :])
                tr.then_inc(row_turned, 1)
            for w in "kv":
                pe.wait_ge(ready[w], 1)

            def body(b):
                need(pe, c_ready, (b + 1) * KC)
                for i in range(KVH):
                    n = b * KVH + i
                    need(pe, k_terms, n - 1)
                    product3(nc, ps_k[i % 2][:, :], [(w_hi["k"][:, c, i * D2:(i + 1) * D2], w_lo["k"][:, c, i * D2:(i + 1) * D2],
                                                      c_hi[:, c, :], c_lo[:, c, :]) for c in range(KC)]).then_inc(k_done, 1)
                    t, h = i // 2, i % 2
                    need(pe, v_copied, n - 1)
                    product3(nc, ps_v[i % 2][:, :], [(c_hi[:, c, t * P:(t + 1) * P], c_lo[:, c, t * P:(t + 1) * P],
                                                      w_hi["v"][:, c, h * BLOCK:(h + 1) * BLOCK], w_lo["v"][:, c, h * BLOCK:(h + 1) * BLOCK])
                                                     for c in range(KC)]).then_inc(v_done, 1)
            blocks(pe, body)


def norm_transposed(nc, stack_type, x, xt_hi, xt_lo, ident, bound, mask_dram):
    with stack_type() as stack:
        m = Memory(nc, stack, "p4_")
        L = statistics_memory(m)
        xn = [m.sb(f"xn{u}", [P, HIDDEN]) for u in range(2)]
        mask = m.sb("mask", [P, TILES, SEQ], I32)
        opened = m.sb("opened", [P, TILES, SEQ])
        ps_t = [m.ps(f"ps_t{u}") for u in range(2)]
        mask_in, masked = m.sem("mask_in"), m.sem("masked")
        xn_ready, transposed, all_hi, all_lo = (m.sem(n) for n in ("xn_ready", "transposed", "all_hi", "all_lo"))

        def tiles(engine, body):
            body(0, 0)
            body(1, 1)
            with engine.Fori(1, TILES // 2 - 1) as i:
                body(i * 2, 0)
                body(i * 2 + 1, 1)
            body(TILES - 2, 0)
            body(TILES - 1, 1)
        block = stack.enter_context(nc.Block())

        @block.sync
        def _(sp):
            sp.dma_start(mask[:, :, :], mask_dram).then_inc(mask_in, 16)

        @block.scalar
        def _(act):
            statistics_scalar(nc, act, L)

            def body(n, u):
                need(act, transposed, n + 1)
                nc.scalar.activation(xt_hi[:, :, ds(n * P, P)], ps_t[u][:, :].rearrange("p (c n) -> p c n", c=KC), ACT.Copy).then_inc(all_hi, 1)
            tiles(act, body)

        @block.vector
        def _(dve):
            statistics_vector(nc, dve, x, L)

            def norm(n, u):
                need(dve, transposed, n - 1)
                normalise(nc, xn[u][:, :], x, L, n).then_inc(xn_ready, 1)
            norm(0, 0)

            def body(n, u):
                if exists(n + 1, TILES):
                    norm(n + 1, 1 - u)
                need(dve, all_hi, n + 1)
                nc.vector.tensor_tensor(xt_lo[:, :, ds(n * P, P)], ps_t[u][:, :].rearrange("p (c n) -> p c n", c=KC),
                                        xt_hi[:, :, ds(n * P, P)], ALU.subtract).then_inc(all_lo, 1)
            tiles(dve, body)
            dve.wait_ge(mask_in, 16)
            nc.vector.tensor_scalar(opened[:, :, :], mask[:, :, :], 0, OPEN, ALU.not_equal, ALU.mult).then_inc(masked, 1)
            nc.vector.tensor_scalar(bound[:, :, :], mask[:, :, :], 0, MASKED, ALU.is_equal, ALU.mult).then_inc(masked, 1)
            dve.wait_ge(masked, 2)
            nc.vector.tensor_tensor(bound[:, :, :], bound[:, :, :], opened[:, :, :], ALU.add).then_inc(masked, 1)

        @block.tensor
        def _(pe):
            def body(n, u):
                need(pe, xn_ready, n + 1)
                need(pe, all_lo, n - 1)
                transpose_chunks(nc, ps_t[u], xn[u], ident).then_inc(transposed, 1)
            tiles(pe, body)


def cross_attention(nc, stack_type, x, xt_hi, xt_lo, cos_t, sin_t, bound, ident, wq_dram, wo_dram, k_scr, v_scr):
    with stack_type() as stack:
        m = Memory(nc, stack, "p5_")
        SCALE = 1.0 / float(np.sqrt(np.float32(D2)))
        ITS, H = KVH * NB, HPG2
        raw = {w: [m.sb(f"raw_{w}{i}", [P, HIDDEN]) for i in range(2)] for w in "qo"}
        w_hi = {w: [m.sb(f"w{w}_hi{h}", [P, HIDDEN], F32R) for h in range(H)] for w in "qo"}
        w_lo = {w: [m.sb(f"w{w}_lo{h}", [P, HIDDEN], F32R) for h in range(H)] for w in "qo"}
        k_t = m.sb("k_t", [P, 2, BLOCK])
        v_in = m.sb("v_in", [P, 2, BLOCK])
        v = m.sb("v", [P, BLOCK])
        q_rot = [m.sb(f"q_rot{h}", [P, BLOCK]) for h in range(H)]
        ra, rb = m.sb("ra", [P, BLOCK]), m.sb("rb", [P, BLOCK])
        s = [m.sb(f"s{i}", [P, TPB, SEQ]) for i in range(2)]
        p = [m.sb(f"p{i}", [P, TPB, SEQ]) for i in range(2)]
        pd = [m.sb(f"pd{i}", [P, TPB, P]) for i in range(2)]
        pt = [m.sb(f"pt{i}", [P, BLOCK]) for i in range(2)]
        mx = [m.sb(f"mx{i}", [P, TPB]) for i in range(2)]
        shift_by = [m.sb(f"shift{i}", [P, TPB]) for i in range(2)]
        total = [m.sb(f"total{i}", [P, TPB]) for i in range(2)]
        inv = [m.sb(f"inv{i}", [P, TPB]) for i in range(2)]
        o_hi = [m.sb(f"o_hi{i}", [P, BLOCK], F32R) for i in range(2)]
        o_lo = [m.sb(f"o_lo{i}", [P, BLOCK], F32R) for i in range(2)]
        ps_q, ps_s, ps_p, ps_o = m.ps("ps_q"), m.ps("ps_s"), m.ps("ps_p"), m.ps("ps_o")
        ps_y = [m.ps(f"ps_y{t}") for t in range(TPB)]
        raw_in = {w: [m.sem(f"raw_in_{w}{i}") for i in range(2)] for w in "qo"}
        part_hi, ready = {w: m.sem(f"part_hi_{w}") for w in "qo"}, {w: m.sem(f"ready_{w}") for w in "qo"}
        k_in, v_loaded, v_ready, zeroed = m.sem("k_in"), m.sem("v_loaded"), m.sem("v_ready"), m.sem("zeroed")
        q_done, q_terms, q_added = m.sem("q_done"), m.sem("q_terms"), m.sem("q_added")
        s_done, s_bound, s_max, s_shift = m.sem("s_done"), m.sem("s_bound"), m.sem("s_max"), m.sem("s_shift")
        p_exp, p_inv, p_norm, p_turned, pt_copied = (m.sem(n) for n in ("p_exp", "p_inv", "p_norm", "p_turned", "pt_copied"))
        pv_done, out_hi, out_lo, y_done, y_added = (m.sem(n) for n in ("pv_done", "out_hi", "out_lo", "y_done", "y_added"))
        block = stack.enter_context(nc.Block())

        def is_last(b):
            return isinstance(b, int) and b == NB - 1

        def is_first(b):
            return isinstance(b, int) and b == 0

        def ahead(g, b, h, k):
            if h + k < H:
                return g, b, g * NB + b, h + k
            if is_last(b):
                return g + 1, 0, (g + 1) * NB, h + k - H
            return g, b + 1, g * NB + b + 1, h + k - H

        @block.sync
        def _(sp):
            def load_weights(g, h):
                need(sp, ready["q"], 4 * g + h - 1)
                sp.dma_start(raw["q"][h % 2][:, :].rearrange("p (c d) -> p c d", c=KC),
                             wq_dram[:, :, ds((g * H + h) * D2, D2)]).then_inc(raw_in["q"][h % 2], 16)
                need(sp, ready["o"], 4 * g + h - 1)
                sp.dma_start(raw["o"][h % 2][:, :], wo_dram[ds((g * H + h) * D2, D2), :]).then_inc(raw_in["o"][h % 2], 16)

            def body(g, b):
                it = g * NB + b
                if is_last(b) and exists(g + 1, KVH):
                    for h in (2, 3):
                        load_weights(g + 1, h)
                if is_first(b) and exists(g + 1, KVH):
                    for h in (0, 1):
                        load_weights(g + 1, h)

            load_weights(0, 0)
            load_weights(0, 1)
            load_weights(0, 2)
            load_weights(0, 3)
            walk(sp, KVH, body)

        def split_hi(act, w, g, h, after, count):
            need(act, raw_in[w][h % 2], (2 * g + h // 2 + 1) * 16)
            need(act, after, count)
            nc.scalar.activation(w_hi[w][h][:, :], raw[w][h % 2][:, :], ACT.Copy).then_inc(part_hi[w], 1)

        def split_lo(pool, w, g, h):
            need(pool, part_hi[w], 4 * g + h + 1)
            nc.gpsimd.tensor_tensor(w_lo[w][h][:, :], raw[w][h % 2][:, :], w_hi[w][h][:, :], ALU.subtract).then_inc(ready[w], 1)

        def refresh(g, b, h):
            it, out = g * NB + b, []
            if is_last(b) and exists(g + 1, KVH):
                out.append(("q", g + 1, h, q_done, it * H + h + 1))
                if h >= 2:
                    out.append(("o", g + 1, h - 2, y_done, (it * H + h - 1) * TPB))
            if is_first(b) and h < 2 and not (isinstance(g, int) and g == 0):
                out.append(("o", g, h + 2, y_done, (it * H + h - 1) * TPB))
            return out

        @block.tensor
        def _(pe):
            def queries(g, b, it, h):
                need(pe, ready["q"], 4 * g + h + 1)
                need(pe, q_terms, it * H + h)
                product3(nc, ps_q[:, :], [(w_hi["q"][h][:, c * P:(c + 1) * P], w_lo["q"][h][:, c * P:(c + 1) * P],
                                           xt_hi[:, c, ds(b * BLOCK, BLOCK)], xt_lo[:, c, ds(b * BLOCK, BLOCK)])
                                          for c in range(KC)]).then_inc(q_done, 1)

            def scores(g, b, it, h):
                n = it * H + h
                need(pe, q_added, n + 1)
                need(pe, k_in, (it + 1) * 16)
                need(pe, s_bound, n)
                for t in range(TPB):
                    mm = nc.tensor.matmul(ps_s[:, t * P:(t + 1) * P], q_rot[h][:, t * P:(t + 1) * P],
                                          k_t[:, ds(it % 2, 1), t * P:(t + 1) * P].squeeze(1), start=True, stop=True)
                mm.then_inc(s_done, 1)

            def turn(it, h):
                n = it * H + h
                need(pe, p_norm, n + 1)
                need(pe, pt_copied, n)
                for t in range(TPB):
                    tr = nc.tensor.transpose(ps_p[:, t * P:(t + 1) * P], pd[h % 2][:, t, :], ident[:, :])
                tr.then_inc(p_turned, 1)

            def mix(it, h):
                n = it * H + h
                if h == 0:
                    need(pe, v_ready, it + 1)
                need(pe, pt_copied, n + 1)
                need(pe, out_lo, n)
                for t in range(TPB):
                    mm = nc.tensor.matmul(ps_o[:, t * P:(t + 1) * P], v[:, t * P:(t + 1) * P],
                                          pt[h % 2][:, t * P:(t + 1) * P], start=True, stop=True)
                mm.then_inc(pv_done, 1)

            def output(g, it, h):
                n = it * H + h
                need(pe, out_lo, n + 1)
                need(pe, ready["o"], 4 * g + h + 1)
                for t in range(TPB):
                    if h == 0:
                        need(pe, y_added, (it - 1) * TPB + t + 1)
                    tile = slice(t * P, (t + 1) * P)
                    nc.tensor.matmul(ps_y[t][:, :], o_hi[h % 2][:, tile], w_hi["o"][h][:, :], start=(h == 0), stop=False)
                    nc.tensor.matmul(ps_y[t][:, :], o_hi[h % 2][:, tile], w_lo["o"][h][:, :], start=False, stop=False)
                    nc.tensor.matmul(ps_y[t][:, :], o_lo[h % 2][:, tile], w_hi["o"][h][:, :], start=False,
                                     stop=(h == H - 1)).then_inc(y_done, 1)

            def body(g, b):
                it = g * NB + b
                for h in range(H):
                    g1, b1, it1, h1 = ahead(g, b, h, 1)
                    if exists(it1, ITS):
                        scores(g1, b1, it1, h1)
                    g2, b2, it2, h2 = ahead(g, b, h, 2)
                    if exists(it2, ITS):
                        queries(g2, b2, it2, h2)
                    turn(it, h)
                    if h > 0:
                        output(g, it, h - 1)
                    elif exists(it - 1, ITS):
                        output(g - 1 if is_first(b) else g, it - 1, H - 1)
                    mix(it, h)

            queries(0, 0, 0, 0)
            queries(0, 0, 0, 1)
            scores(0, 0, 0, 0)
            walk(pe, KVH, body)
            output(KVH - 1, ITS - 1, H - 1)

        @block.scalar
        def _(act):
            def load_kv(g, b, it):
                need(act, k_in, it * 16)
                need(act, s_done, (it - 1) * H)
                act.dma_start(k_t[:, ds(it % 2, 1), :], k_scr[ds(g, 1), ds(b, 1), :, :].rearrange("g b p n -> p (g b) n")).then_inc(k_in, 16)
                need(act, v_loaded, it * 16)
                need(act, v_ready, it - 1)
                act.dma_start(v_in[:, ds(it % 2, 1), :], v_scr[ds(g, 1), ds(b, 1), :, :, :].rearrange("g b p t d -> p (g b) (t d)")).then_inc(v_loaded, 16)

            def exponentials(it, h):
                n = it * H + h
                need(act, s_shift, n + 1)
                need(act, p_norm, n - 1)
                for t in range(TPB):
                    e = nc.scalar.activation(p[h % 2][:, t, :], s[h % 2][:, t, :], ACT.Exp, bias=shift_by[h % 2][:, t:t + 1],
                                             scale=SCALE, accum_out=total[h % 2][:, t:t + 1])
                e.then_inc(p_exp, 1)

            def copy_turned(it, h):
                n = it * H + h
                need(act, p_turned, n + 1)
                need(act, pv_done, n - 1)
                nc.scalar.activation(pt[h % 2][:, :], ps_p[:, :], ACT.Copy).then_inc(pt_copied, 1)

            def outputs_hi(it, h):
                n = it * H + h
                need(act, pv_done, n + 1)
                need(act, y_done, (n - 1) * TPB)
                nc.scalar.activation(o_hi[h % 2][:, :], ps_o[:, :], ACT.Copy).then_inc(out_hi, 1)

            def body(g, b):
                it = g * NB + b
                for h in range(H):
                    if h > 0:
                        outputs_hi(it, h - 1)
                    elif exists(it - 1, ITS):
                        outputs_hi(it - 1, H - 1)
                    _, _, it1, h1 = ahead(g, b, h, 1)
                    if exists(it1, ITS):
                        exponentials(it1, h1)
                    copy_turned(it, h)
                    if h == 1 and exists(it + 1, ITS):
                        load_kv(*ahead(g, b, H - 1, 1)[:3])
                    for w, gw, hw, after, count in refresh(g, b, h):
                        split_hi(act, w, gw, hw, after, count)

            load_kv(0, 0, 0)
            for h in range(H):
                split_hi(act, "q", 0, h, q_done, 0)
                split_hi(act, "o", 0, h, y_done, 0)
            exponentials(0, 0)
            walk(act, KVH, body)
            outputs_hi(ITS - 1, H - 1)

        @block.vector
        def _(dve):
            def maxima(b, it, h):
                n = it * H + h
                sc = ps_s[:, :].rearrange("p (t k) -> p t k", t=TPB)
                need(dve, s_done, n + 1)
                need(dve, p_exp, n - 1)
                for r in range(2):
                    rows = slice(r * SEQ, (r + 1) * SEQ)
                    low = nc.vector.tensor_tensor(s[h % 2][rows, :, :], sc[rows, :, rows], bound[rows, ds(b * TPB, TPB), :], ALU.min)
                low.then_inc(s_bound, 1)
                need(dve, s_bound, n + 1)
                nc.vector.tensor_reduce(mx[h % 2][:, :], s[h % 2][:, :, :], AX.X, ALU.max).then_inc(s_max, 1)
                need(dve, s_max, n + 1)
                nc.vector.tensor_scalar(shift_by[h % 2][:, :], mx[h % 2][:, :], -SCALE, None, ALU.mult).then_inc(s_shift, 1)

            def invert(it, h):
                need(dve, p_exp, it * H + h + 1)
                nc.vector.reciprocal(inv[h % 2][:, :], total[h % 2][:, :]).then_inc(p_inv, 1)

            def rotate(b, it, h):
                n = it * H + h
                need(dve, q_done, n + 1)
                need(dve, q_added, n)
                rotate_terms(nc, ps_q, cos_t[:, ds(b * BLOCK, BLOCK)], sin_t[:, ds(b * BLOCK, BLOCK)], ra, rb).then_inc(q_terms, 1)

            def outputs_lo(it, h):
                need(dve, out_hi, it * H + h + 1)
                nc.vector.tensor_tensor(o_lo[h % 2][:, :], ps_o[:, :], o_hi[h % 2][:, :], ALU.subtract).then_inc(out_lo, 1)

            def copy_values(it):
                need(dve, v_loaded, (it + 1) * 16)
                need(dve, pv_done, it * H)
                nc.vector.tensor_copy(v[:, :].unsqueeze(1), v_in[:, ds(it % 2, 1), :]).then_inc(v_ready, 1)

            def add(b, it, tiles):
                for t in tiles:
                    need(dve, y_done, (it * H + H - 1) * TPB + t + 1)
                    need(dve, y_added, it * TPB + t)
                    xs = x[:, ds(b * TPB + t, 1), :]
                    nc.vector.tensor_tensor(xs, ps_y[t][:, :].unsqueeze(1), xs, ALU.add).then_inc(y_added, 1)

            def body(g, b):
                it = g * NB + b
                for h in range(H):
                    if h > 0:
                        outputs_lo(it, h - 1)
                    else:
                        if exists(it - 1, ITS):
                            outputs_lo(it - 1, H - 1)
                        copy_values(it)
                    _, b1, it1, h1 = ahead(g, b, h, 1)
                    if exists(it1, ITS):
                        maxima(b1, it1, h1)
                    _, b2, it2, h2 = ahead(g, b, h, 2)
                    if h == 1 and exists(it - 1, ITS):
                        add(NB - 1 if is_first(b) else b - 1, it - 1, (2, 3))
                    if exists(it2, ITS):
                        rotate(b2, it2, h2)
                    if exists(it1, ITS):
                        invert(it1, h1)
                    if h == 0 and exists(it - 1, ITS):
                        add(NB - 1 if is_first(b) else b - 1, it - 1, (0, 1))

            for i in range(2):
                nc.vector.memset(pd[i][:, :, :], 0.0).then_inc(zeroed, 1)
            rotate(0, 0, 0)
            rotate(0, 0, 1)
            maxima(0, 0, 0)
            invert(0, 0)
            walk(dve, KVH, body)
            outputs_lo(ITS - 1, H - 1)
            add(NB - 1, ITS - 1, range(TPB))

        @block.gpsimd
        def _(pool):
            def normalise_p(it, h):
                n = it * H + h
                need(pool, p_inv, n + 1)
                need(pool, p_turned, n - 1)
                need(pool, q_added, min(n + 2, ITS * H) if isinstance(n, int) else n + 2)
                for r in range(2):
                    rows = slice(r * SEQ, (r + 1) * SEQ)
                    mul = nc.gpsimd.tensor_tensor(pd[h % 2][rows, :, rows], p[h % 2][rows, :, :],
                                                  inv[h % 2][rows, :].unsqueeze(2).broadcast_to([SEQ, TPB, SEQ]), ALU.mult)
                mul.then_inc(p_norm, 1)

            def add_terms(it, h):
                n = it * H + h
                need(pool, q_terms, n + 1)
                need(pool, s_done, n + 1 - H)
                need(pool, p_norm, n - 1)
                nc.gpsimd.tensor_tensor(q_rot[h][:, :], ra[:, :], rb[:, :], ALU.add).then_inc(q_added, 1)

            def body(g, b):
                for h in range(H):
                    _, _, it1, h1 = ahead(g, b, h, 1)
                    _, _, it2, h2 = ahead(g, b, h, 2)
                    if exists(it2, ITS):
                        add_terms(it2, h2)
                    for w, gw, hw, _, _ in refresh(g, b, h):
                        split_lo(pool, w, gw, hw)
                        need(pool, ready[w], 4 * gw + hw + 1)
                    if exists(it1, ITS):
                        normalise_p(it1, h1)

            for h in range(H):
                split_lo(pool, "q", 0, h)
                split_lo(pool, "o", 0, h)
            add_terms(0, 0)
            add_terms(0, 1)
            pool.wait_ge(zeroed, 2)
            normalise_p(0, 0)
            walk(pool, KVH, body)


def lora_linear(nc, stack_type, x, ident, gate_dram, eye_dram, la_dram, lb_dram, as_dram, bs_dram, w_dram, bias_dram, out_dram):
    with stack_type() as stack:
        m = Memory(nc, stack, "p6_")
        L = statistics_memory(m)
        GT = TILES // LB
        GTOK = GT * P
        gate, eye = m.sb("gate", [P, NCH, LB]), m.sb("eye", [P, RANK])
        pick = m.sb("pick", [P, NCH, LB, RANK])
        la, lb = m.sb("la", [P, NCH, HIDDEN]), m.sb("lb", [P, NCH, HIDDEN])
        a_all = m.sb("a_all", [P, KC, LB * RANK])
        as_raw = m.sb("as_raw", [P, KC, RANK])
        bs_raw = m.sb("bs_raw", [2 * RANK, HIDDEN])
        a_hi, a_lo = m.sb("a_hi", [P, KC, P], F32R), m.sb("a_lo", [P, KC, P], F32R)
        b_hi, b_lo = m.sb("b_hi", [P, LB, HIDDEN], F32R), m.sb("b_lo", [P, LB, HIDDEN], F32R)
        w_raw = m.sb("w_raw", [P, KC, HIDDEN])
        w_hi, w_lo = m.sb("w_hi", [P, KC, HIDDEN], F32R), m.sb("w_lo", [P, KC, HIDDEN], F32R)
        bias = m.sb("bias", [P, HIDDEN])
        xn = [m.sb(f"xn{u}", [P, HIDDEN]) for u in range(2)]
        t_hi = [m.sb(f"t_hi{q}", [P, KC, GTOK], F32R) for q in range(2)]
        t_lo = [m.sb(f"t_lo{q}", [P, KC, GTOK], F32R) for q in range(2)]
        r_hi, r_lo = m.sb("r_hi", [P, GTOK], F32R), m.sb("r_lo", [P, GTOK], F32R)
        y = [m.sb(f"y{u}", [P, HIDDEN]) for u in range(2)]
        yb = [m.sb(f"yb{u}", [P, HIDDEN]) for u in range(2)]
        ps_t = [m.ps(f"ps_t{u}") for u in range(2)]
        ps_y = [m.ps(f"ps_y{u}") for u in range(2)]
        ps_r = m.ps("ps_r")
        ps_a = [m.ps(f"ps_a{i}") for i in range(2)]
        loads = {n: m.sem(n + "_in") for n in ("gate", "eye", "la", "lb", "sa", "sb", "w", "bias")}
        zeroed, picked, w_part, w_ready = m.sem("zeroed"), m.sem("picked"), m.sem("w_part"), m.sem("w_ready")
        a_done, a_copied, bm_done, b_part, b_ready = (m.sem(n) for n in ("a_done", "a_copied", "bm_done", "b_part", "b_ready"))
        shared_hi, shared_ready = m.sem("shared_hi"), m.sem("shared_ready")
        xn_ready, transposed, tile_hi, tile_lo = (m.sem(n) for n in ("xn_ready", "transposed", "tile_hi", "tile_lo"))
        ag_hi, ag_ready, r_done, rank_hi, rank_lo = (m.sem(n) for n in ("ag_hi", "ag_ready", "r_done", "rank_hi", "rank_lo"))
        y_done, y_added, y_biased = m.sem("y_done"), m.sem("y_added"), m.sem("y_biased")
        stored = [m.sem(f"stored{u}") for u in range(2)]

        def groups(engine, body):
            body(0, 0)
            body(1, 1)
            with engine.Fori(1, LB // 2 - 1) as i:
                body(i * 2, 0)
                body(i * 2 + 1, 1)
            body(LB - 2, 0)
            body(LB - 1, 1)
        block = stack.enter_context(nc.Block())

        @block.sync
        def _(sp):
            for k in range(NPC):
                sp.dma_start(gate[k * RANK:(k + 1) * RANK, :, :], gate_dram[k, :, :].unsqueeze(0).broadcast_to([RANK, NCH, LB])).then_inc(loads["gate"], 16)
            sp.dma_start(eye[:, :], eye_dram).then_inc(loads["eye"], 16)
            sp.dma_start(la[:, :, :], la_dram).then_inc(loads["la"], 16)
            sp.dma_start(lb[:, :, :], lb_dram).then_inc(loads["lb"], 16)
            sp.dma_start(as_raw[:, :, :], as_dram).then_inc(loads["sa"], 16)
            sp.dma_start(bs_raw[RANK:2 * RANK, :], bs_dram).then_inc(loads["sb"], 16)
            sp.dma_start(w_raw[:, :, :], w_dram).then_inc(loads["w"], 16)
            sp.dma_start(bias[:, :], bias_dram.broadcast_to([P, HIDDEN])).then_inc(loads["bias"], 16)

            def body(n, q):
                for u in range(GT):
                    t = n * GT + u
                    need(sp, y_biased, t + 1)
                    sp.dma_start(out_dram[:, ds(t, 1), :], yb[u][:, :].unsqueeze(1)).then_inc(stored[u], 16)
            groups(sp, body)
            for u in range(GT):
                sp.wait_ge(stored[u], 16 * LB)

        @block.gpsimd
        def _(pool):
            nc.gpsimd.memset(b_hi[:, :, :].bitcast(F32), 0.0).then_inc(zeroed, 1)
            nc.gpsimd.memset(b_lo[:, :, :].bitcast(F32), 0.0).then_inc(zeroed, 1)
            pool.wait_ge(loads["bias"], 16)

            def body(n, q):
                for u in range(GT):
                    t = n * GT + u
                    need(pool, y_added, t + 1)
                    need(pool, stored[u], n * 16)
                    nc.gpsimd.tensor_tensor(yb[u][:, :], y[u][:, :], bias[:, :], ALU.add).then_inc(y_biased, 1)
            groups(pool, body)

        @block.scalar
        def _(act):
            statistics_scalar(nc, act, L)
            act.wait_ge(loads["w"], 16)
            nc.scalar.activation(w_hi[:, :, :], w_raw[:, :, :], ACT.Copy).then_inc(w_part, 1)
            for c in range(KC):
                act.wait_ge(a_done, c + 1)
                nc.scalar.activation(a_all[:, c, :], ps_a[c % 2][:, 0:LB * RANK], ACT.Copy).then_inc(a_copied, 1)
            act.wait_ge(zeroed, 4)
            for b in range(LB):
                act.wait_ge(bm_done, b // NPC + 1)
                src = ps_a[b // NPC][(b % NPC) * RANK:(b % NPC + 1) * RANK, :]
                nc.scalar.activation(b_hi[0:RANK, b, :], src, ACT.Copy).then_inc(b_part, 1)
            act.wait_ge(loads["sa"], 16)
            act.wait_ge(loads["sb"], 16)
            nc.scalar.activation(a_hi[:, :, RANK:2 * RANK], as_raw[:, :, :], ACT.Copy).then_inc(shared_hi, 1)
            nc.scalar.activation(b_hi[RANK:2 * RANK, :, :], bs_raw[RANK:2 * RANK, :].unsqueeze(1).broadcast_to([RANK, LB, HIDDEN]),
                                 ACT.Copy).then_inc(shared_hi, 1)

            def rank_parts(n):
                need(act, r_done, n + 1)
                need(act, y_done, n * GT)
                nc.scalar.activation(r_hi[:, :], ps_r[:, 0:GTOK], ACT.Copy).then_inc(rank_hi, 1)

            def body(n, q):
                for u in range(GT):
                    t = n * GT + u
                    need(act, transposed, t + 1)
                    need(act, y_done, (n - 1) * GT)
                    nc.scalar.activation(t_hi[q][:, :, u * P:(u + 1) * P], ps_t[u][:, :].rearrange("p (c n) -> p c n", c=KC), ACT.Copy).then_inc(tile_hi, 1)
                need(act, r_done, n)
                nc.scalar.activation(a_hi[:, :, 0:RANK], a_all[:, :, ds(n * RANK, RANK)], ACT.Copy).then_inc(ag_hi, 1)
                if exists(n - 1, LB):
                    rank_parts(n - 1)
            act.wait_ge(a_copied, KC)
            groups(act, body)
            rank_parts(LB - 1)

        @block.vector
        def _(dve):
            nc.vector.memset(a_hi[:, :, :].bitcast(F32), 0.0).then_inc(zeroed, 1)
            nc.vector.memset(a_lo[:, :, :].bitcast(F32), 0.0).then_inc(zeroed, 1)
            statistics_vector(nc, dve, x, L)
            dve.wait_ge(loads["gate"], 16 * NPC)
            dve.wait_ge(loads["eye"], 16)
            for k in range(NCH):
                nc.vector.tensor_tensor(pick[:, k, :, :], gate[:, k, :].unsqueeze(2).broadcast_to([P, LB, RANK]),
                                        eye[:, :].unsqueeze(1).broadcast_to([P, LB, RANK]), ALU.mult).then_inc(picked, 1)
            dve.wait_ge(w_part, 1)
            nc.vector.tensor_tensor(w_lo[:, :, :], w_raw[:, :, :], w_hi[:, :, :], ALU.subtract).then_inc(w_ready, 1)
            dve.wait_ge(zeroed, 4)
            for b in range(LB):
                dve.wait_ge(b_part, b + 1)
                src = ps_a[b // NPC][(b % NPC) * RANK:(b % NPC + 1) * RANK, :]
                nc.vector.tensor_tensor(b_lo[0:RANK, b, :], src, b_hi[0:RANK, b, :], ALU.subtract).then_inc(b_ready, 1)
            dve.wait_ge(shared_hi, 2)
            nc.vector.tensor_tensor(a_lo[:, :, RANK:2 * RANK], as_raw[:, :, :], a_hi[:, :, RANK:2 * RANK], ALU.subtract).then_inc(shared_ready, 1)
            nc.vector.tensor_tensor(b_lo[RANK:2 * RANK, :, :], bs_raw[RANK:2 * RANK, :].unsqueeze(1).broadcast_to([RANK, LB, HIDDEN]),
                                    b_hi[RANK:2 * RANK, :, :], ALU.subtract).then_inc(shared_ready, 1)

            def norm(t, u):
                need(dve, transposed, t - 1)
                normalise(nc, xn[u][:, :], x, L, t).then_inc(xn_ready, 1)

            def rank_parts(n):
                need(dve, rank_hi, n + 1)
                nc.vector.tensor_tensor(r_lo[:, :], ps_r[:, 0:GTOK], r_hi[:, :], ALU.subtract).then_inc(rank_lo, 1)

            def add(n):
                for u in range(GT):
                    t = n * GT + u
                    need(dve, y_done, t + 1)
                    need(dve, y_biased, t - 1)
                    nc.vector.tensor_tensor(y[u][:, :].unsqueeze(1), ps_y[u][:, :].unsqueeze(1), x[:, ds(t, 1), :], ALU.add).then_inc(y_added, 1)

            def body(n, q):
                for u in range(GT):
                    norm(n * GT + u, u)
                for u in range(GT):
                    t = n * GT + u
                    need(dve, tile_hi, t + 1)
                    nc.vector.tensor_tensor(t_lo[q][:, :, u * P:(u + 1) * P], ps_t[u][:, :].rearrange("p (c n) -> p c n", c=KC),
                                            t_hi[q][:, :, u * P:(u + 1) * P], ALU.subtract).then_inc(tile_lo, 1)
                need(dve, ag_hi, n + 1)
                nc.vector.tensor_tensor(a_lo[:, :, 0:RANK], a_all[:, :, ds(n * RANK, RANK)], a_hi[:, :, 0:RANK], ALU.subtract).then_inc(ag_ready, 1)
                if exists(n - 1, LB):
                    rank_parts(n - 1)
                    add(n - 1)
            groups(dve, body)
            rank_parts(LB - 1)
            add(LB - 1)

        @block.tensor
        def _(pe):
            pe.wait_ge(picked, NCH)
            pe.wait_ge(loads["la"], 16)
            for c in range(KC):
                need(pe, a_copied, c - 1)
                for k in range(NCH):
                    mm = nc.tensor.matmul(ps_a[c % 2][:, 0:LB * RANK], la[:, k, c * P:(c + 1) * P],
                                          pick[:, k, :, :].rearrange("p b r -> p (b r)"), start=(k == 0), stop=(k == NCH - 1))
                mm.then_inc(a_done, 1)
            pe.wait_ge(loads["lb"], 16)
            pe.wait_ge(a_copied, KC)
            for half in range(LB // NPC):
                for k in range(NCH):
                    mm = nc.tensor.matmul(ps_a[half][:, :], pick[:, k, half * NPC:(half + 1) * NPC, :].rearrange("p b r -> p (b r)"),
                                          lb[:, k, :], start=(k == 0), stop=(k == NCH - 1))
                mm.then_inc(bm_done, 1)

            def ranks(n, q):
                need(pe, tile_lo, (n + 1) * GT)
                need(pe, ag_ready, n + 1)
                need(pe, rank_lo, n)
                product3(nc, ps_r[:, 0:GTOK], [(a_hi[:, c, :], a_lo[:, c, :], t_hi[q][:, c, :], t_lo[q][:, c, :])
                                               for c in range(KC)]).then_inc(r_done, 1)

            def linear(n, q):
                for u in range(GT):
                    t, tile = n * GT + u, slice(u * P, (u + 1) * P)
                    need(pe, y_added, t - 1)
                    for c in range(KC):
                        nc.tensor.matmul(ps_y[u][:, :], t_hi[q][:, c, tile], w_hi[:, c, :], start=(c == 0), stop=False)
                        nc.tensor.matmul(ps_y[u][:, :], t_hi[q][:, c, tile], w_lo[:, c, :], start=False, stop=False)
                        nc.tensor.matmul(ps_y[u][:, :], t_lo[q][:, c, tile], w_hi[:, c, :], start=False, stop=False)
                    if u == 0:
                        need(pe, rank_lo, n + 1)
                    bh, bl = b_hi[:, ds(n, 1), :].squeeze(1), b_lo[:, ds(n, 1), :].squeeze(1)
                    nc.tensor.matmul(ps_y[u][:, :], r_hi[:, tile], bh, start=False, stop=False)
                    nc.tensor.matmul(ps_y[u][:, :], r_hi[:, tile], bl, start=False, stop=False)
                    nc.tensor.matmul(ps_y[u][:, :], r_lo[:, tile], bh, start=False, stop=True).then_inc(y_done, 1)

            pe.wait_ge(w_ready, 1)
            pe.wait_ge(b_ready, LB)
            pe.wait_ge(shared_ready, 2)

            def body(n, q):
                for u in range(GT):
                    t = n * GT + u
                    need(pe, xn_ready, t + 1)
                    need(pe, tile_lo, t - 1)
                    transpose_chunks(nc, ps_t[u], xn[u], ident).then_inc(transposed, 1)
                if exists(n - 1, LB):
                    linear(n - 1, 1 - q)
                ranks(n, q)
            groups(pe, body)
            linear(LB - 1, 1)


def decoder_layer(nc, stack_type, x, ctx, pos, mask, wq1, wk1, wv1, wo1, wq2, wk2, wv2, wo2, gate, wf, bias, la, lb, las, lbs,
                  ident_c, heads_c, eye_c, table_c, out):
    by_chunk = "(c p) n -> p c n"
    by_tile = "(t p) n -> p t n"
    with stack_type() as stack:
        m = Memory(nc, stack, "")
        k_scr = nc.dram_tensor("k_scratch", (KVH, NB, P, BLOCK), F32, kind="Internal").ap()
        v_scr = nc.dram_tensor("v_scratch", (KVH, NB, P, TPB, D2), F32, kind="Internal").ap()
        xs, ident = m.sb("x_sb", [P, TILES, HIDDEN]), m.sb("ident", [P, P])
        with stack_type() as inner:
            mi = Memory(nc, inner, "a_")
            xt_hi, xt_lo = mi.sb("xt_hi", [P, KC, TOKENS], F32R), mi.sb("xt_lo", [P, KC, TOKENS], F32R)
            v1 = mi.sb("v1", [P, TILES, HIDDEN])
            norm_and_values(nc, stack_type, xs, xt_hi, xt_lo, v1, ident, x.rearrange(by_tile, p=P), wv1.rearrange(by_chunk, p=P), ident_c)
            self_attention(nc, stack_type, xs, xt_hi, xt_lo, v1, ident, wq1.rearrange(by_chunk, p=P), wk1.rearrange(by_chunk, p=P), wo1, heads_c)
        with stack_type() as inner:
            mi = Memory(nc, inner, "b_")
            cos_t, sin_t = mi.sb("cos_t", [P, TOKENS]), mi.sb("sin_t", [P, TOKENS])
            keys_and_values(nc, stack_type, cos_t, sin_t, ident, pos, table_c, ctx.rearrange(by_chunk, p=P),
                            wk2.rearrange(by_chunk, p=P), wv2.rearrange(by_chunk, p=P), k_scr, v_scr)
            bound = mi.sb("bound", [P, TILES, SEQ])
            xt_hi, xt_lo = mi.sb("xt_hi", [P, KC, TOKENS], F32R), mi.sb("xt_lo", [P, KC, TOKENS], F32R)
            norm_transposed(nc, stack_type, xs, xt_hi, xt_lo, ident, bound, mask.rearrange(by_tile, p=P))
            cross_attention(nc, stack_type, xs, xt_hi, xt_lo, cos_t, sin_t, bound, ident, wq2.rearrange(by_chunk, p=P), wo2, k_scr, v_scr)
        lora_linear(nc, stack_type, xs, ident, gate, eye_c, la.rearrange("(k q) n -> q k n", q=P), lb.rearrange("(k q) n -> q k n", q=P),
                    las.rearrange(by_chunk, p=P), lbs, wf.rearrange(by_chunk, p=P), bias, out.rearrange(by_tile, p=P))


def rotary_table():
    inv_freq = (np.float32(1.0) / np.power(np.float32(10000.0), np.arange(0, D2, 2, dtype=np.float32) / np.float32(D2))).astype(np.float32)
    angle = np.arange(MAX_POS, dtype=np.float32)[:, None] * inv_freq[None, :]
    cos, sin = np.cos(angle).astype(np.float32), np.sin(angle).astype(np.float32)
    return np.concatenate([cos, cos, sin, -sin], axis=1)


def kernel(**inputs):
    import concourse.bacc as bacc
    from concourse.bass_utils import run_bass_kernel_spmd
    from contextlib import ExitStack

    a = {k: np.asarray(v) for k, v in inputs.items()}
    arrays = {
        "x": a["x"].reshape(TOKENS, HIDDEN),
        "ctx": a["ctx_4096"].reshape(TOKENS, HIDDEN).T,
        "pos": a["pos_BxS2"].reshape(TILES, P).T,
        "mask": a["mask_BxSxS2_ik0"].reshape(TOKENS, SEQ),
        "wq1": a["L0_attn_w_q"].T, "wk1": a["L0_attn_w_k"].T, "wv1": a["L0_attn_w_v"].T, "wo1": a["L0_attn_w_o"].T,
        "wq2": a["L0_xattn_Wq"], "wk2": a["L0_xattn_Wk"], "wv2": a["L0_xattn_Wv"], "wo2": a["L0_xattn_Wo"],
        "gate": a["L0_ffn_gate"].T.reshape(NCH, NPC, LB).transpose(1, 0, 2),
        "wf": a["L0_ffn_kernel"], "bias": a["L0_ffn_bias"].reshape(1, HIDDEN),
        "la": a["L0_ffn_lora_A"].reshape(NLORA * RANK, HIDDEN),
        "lb": a["L0_ffn_lora_B"].transpose(0, 2, 1).reshape(NLORA * RANK, HIDDEN),
        "las": a["L0_ffn_lora_A_shared"].T, "lbs": a["L0_ffn_lora_B_shared"].T,
        "ident_c": np.eye(P, dtype=np.float32),
        "heads_c": np.repeat(np.eye(HPG1, dtype=np.float32), D1, axis=0),
        "eye_c": np.tile(np.eye(RANK, dtype=np.float32), (NPC, 1)),
        "table_c": rotary_table(),
    }
    nc = bacc.Bacc("TRN2", target_bir_lowering=False, num_devices=1)
    given, args = {}, []
    for name, value in arrays.items():
        value = np.ascontiguousarray(value)
        dt = mybir.dt.uint32 if name == "pos" else mybir.dt.from_np(value.dtype)
        if name == "pos":
            value = value.view(np.uint32)
        given["in_" + name] = value
        args.append(nc.dram_tensor("in_" + name, value.shape, dt, kind="ExternalInput").ap())
    args.append(nc.dram_tensor("out", (TOKENS, HIDDEN), F32, kind="ExternalOutput").ap())
    decoder_layer(nc, ExitStack, *args)
    r = run_bass_kernel_spmd(nc, [given], core_ids=[0])
    return r.results[0]["out"].reshape(BATCH, SEQ, HIDDEN)
```

```python
import numpy as np
import concourse.bass as bass
from concourse import mybir

F32 = mybir.dt.float32
F32R = mybir.dt.float32r
I32 = mybir.dt.int32
ALU = mybir.AluOpType
ACT = mybir.ActivationFunctionType
AX = mybir.AxisListType

P = 128
BATCH, SEQ, HIDDEN = 32, 64, 512
TOKENS = BATCH * SEQ
TILES = TOKENS // P
BLOCK = 512
NB = TOKENS // BLOCK
TPB = BLOCK // P
KC = HIDDEN // P
EPS = 1e-5
H1, D1 = 32, 16
HPG1 = P // D1
G1 = H1 // HPG1
VPITCH = P + D1
VROW = HPG1 * VPITCH
H2, KVH, D2 = 32, 8, 128
HPG2 = H2 // KVH
HALF = D2 // 2
MAX_POS = 512
MASKED = -1e9 * float(np.sqrt(np.float32(D2)))
OPEN = 3.0e38
LB, NLORA, RANK = 8, 16, 32
NPC = P // RANK
NCH = NLORA // NPC


def need(engine, semaphore, value):
    if not isinstance(value, int) or value > 0:
        engine.wait_ge(semaphore, value)


def exists(index, count):
    return not isinstance(index, int) or 0 <= index < count


def ds(start, size):
    return slice(start, start + size) if isinstance(start, int) else bass.ds(start, size)


def product3(nc, out, chunks, before=lambda c: None):
    last = len(chunks) - 1
    for c, (lh, ll, rh, rl) in enumerate(chunks):
        before(c)
        nc.tensor.matmul(out, lh, rh, start=(c == 0), stop=False)
        nc.tensor.matmul(out, lh, rl, start=False, stop=False)
        mm = nc.tensor.matmul(out, ll, rh, start=False, stop=(c == last))
    return mm


def walk(engine, groups, body):
    def row(g):
        body(g, 0)
        with engine.Fori(1, NB - 1) as b:
            body(g, b)
        body(g, NB - 1)
    for b in range(NB):
        body(0, b)
    with engine.Fori(1, groups - 1) as g:
        row(g)
    row(groups - 1)


class Memory:

    def __init__(self, nc, stack, prefix):
        self.nc, self.stack, self.prefix = nc, stack, prefix

    def sb(self, name, shape, dt=F32):
        return self.stack.enter_context(self.nc.sbuf_tensor(self.prefix + name, shape, dt))

    def ps(self, name, shape=(P, 512)):
        return self.stack.enter_context(self.nc.psum_tensor(self.prefix + name, list(shape), F32))

    def sem(self, name):
        return self.stack.enter_context(self.nc.semaphore(self.prefix + name))


class Norm:

    def __init__(self, buffers, semaphores, index):
        self.stats, self.mv, self.sd, self.rstd = buffers
        self.stat, self.var, self.root, self.norm = semaphores
        self.index = index

    def collect(self, nc, t):
        nc.vector.bn_stats(self.stats[:, ds(t, 1), :].squeeze(1) if not isinstance(t, int) else self.stats[:, t, :],
                           self.x[:, ds(t, 1), :].squeeze(1) if not isinstance(t, int) else self.x[:, t, :]).then_inc(self.stat, 1)

    def finish_vector(self, nc, dve):
        dve.wait_ge(self.stat, (self.index + 1) * TILES)
        for t in range(TILES):
            nc.vector.bn_aggr(self.mv[:, t, :], self.stats[:, t, :]).then_inc(self.var, 1)
        dve.wait_ge(self.var, self.index * (TILES + 1) + TILES)
        nc.vector.tensor_scalar(self.sd[:, :], self.mv[:, :, 1], EPS, None, ALU.add).then_inc(self.var, 1)
        dve.wait_ge(self.root, self.index + 1)
        nc.vector.reciprocal(self.rstd[:, :], self.sd[:, :]).then_inc(self.norm, 1)
        dve.wait_ge(self.norm, self.index + 1)

    def finish_scalar(self, nc, act):
        act.wait_ge(self.var, (self.index + 1) * (TILES + 1))
        nc.scalar.activation(self.sd[:, :], self.sd[:, :], ACT.Sqrt).then_inc(self.root, 1)

    def apply(self, nc, out, t):
        return nc.vector.tensor_scalar(out, self.x[:, ds(t, 1), :].squeeze(1) if not isinstance(t, int) else self.x[:, t, :],
                                       self.mv[:, ds(t, 1), 0], self.rstd[:, ds(t, 1)], ALU.subtract, ALU.mult)


def transpose_chunks(nc, out, src, ident):
    for c in range(KC):
        tr = nc.tensor.transpose(out[:, c * P:(c + 1) * P], src[:, c * P:(c + 1) * P], ident[:, :])
    return tr


def norm_and_values(nc, stack_type, norm1, xt_hi, xt_lo, v1, ident, wv_dram):
    with stack_type() as stack:
        m = Memory(nc, stack, "p2_")
        wv_raw = m.sb("wv_raw", [P, KC, HIDDEN])
        wv_hi, wv_lo = (m.sb(n, [P, KC, HIDDEN], F32R) for n in ("wv_hi", "wv_lo"))
        xn = [m.sb(f"xn{u}", [P, HIDDEN]) for u in range(2)]
        t_hi = [m.sb(f"t_hi{u}", [P, KC, P], F32R) for u in range(2)]
        t_lo = [m.sb(f"t_lo{u}", [P, KC, P], F32R) for u in range(2)]
        ps_t = [m.ps(f"ps_t{u}") for u in range(2)]
        ps_v = [m.ps(f"ps_v{u}") for u in range(2)]
        w_in, w_hi, w_ready = m.sem("w_in"), m.sem("w_hi"), m.sem("w_ready")
        xn_ready, transposed = m.sem("xn_ready"), m.sem("transposed")
        all_hi, tile_lo, all_lo = m.sem("all_hi"), m.sem("tile_lo"), m.sem("all_lo")
        v_done, v_copied = m.sem("v_done"), m.sem("v_copied")

        def tiles(engine, body):
            for n in range(4):
                body(n, n % 2)
            with engine.Fori(2, TILES // 2 - 1) as i:
                body(i * 2, 0)
                body(i * 2 + 1, 1)
            body(TILES - 2, 0)
            body(TILES - 1, 1)

        block = stack.enter_context(nc.Block())

        @block.sync
        def _(sp):
            sp.dma_start(wv_raw[:, :, :], wv_dram).then_inc(w_in, 16)

        @block.scalar
        def _(act):
            norm1.finish_scalar(nc, act)

            def copy_values(n):
                need(act, v_done, n + 1)
                nc.scalar.activation(v1[:, ds(n, 1), :], ps_v[slot_of[0]][:, :].unsqueeze(1), ACT.Copy).then_inc(v_copied, 1)

            slot_of = [0]

            def body(n, u):
                need(act, transposed, n + 1)
                need(act, v_done, n - 1)
                nc.scalar.activation(t_hi[u][:, :, :], ps_t[u][:, :].rearrange("p (c n) -> p c n", c=KC), ACT.Copy)
                nc.scalar.activation(xt_hi[:, :, ds(n * P, P)], ps_t[u][:, :].rearrange("p (c n) -> p c n", c=KC), ACT.Copy).then_inc(all_hi, 1)
                slot_of[0] = 1 - u
                if isinstance(n, int) and n == 0:
                    act.wait_ge(w_in, 16)
                    nc.scalar.activation(wv_hi[:, :, :], wv_raw[:, :, :], ACT.Copy).then_inc(w_hi, 1)
                if exists(n - 1, TILES):
                    copy_values(n - 1)
            tiles(act, body)
            slot_of[0] = 1
            copy_values(TILES - 1)

        @block.vector
        def _(dve):
            norm1.finish_vector(nc, dve)

            def norm(n, u):
                need(dve, transposed, n - 1)
                norm1.apply(nc, xn[u][:, :], n).then_inc(xn_ready, 1)

            norm(0, 0)

            def body(n, u):
                if exists(n + 1, TILES):
                    norm(n + 1, 1 - u)
                need(dve, all_hi, n + 1)
                need(dve, all_lo, n - 1)
                nc.vector.tensor_tensor(t_lo[u][:, :, :], ps_t[u][:, :].rearrange("p (c n) -> p c n", c=KC),
                                        t_hi[u][:, :, :], ALU.subtract).then_inc(tile_lo, 1)
                if isinstance(n, int) and n == 0:
                    dve.wait_ge(w_hi, 1)
                    nc.vector.tensor_tensor(wv_lo[:, :, :], wv_raw[:, :, :], wv_hi[:, :, :], ALU.subtract).then_inc(w_ready, 1)
            tiles(dve, body)

        @block.gpsimd
        def _(pool):
            def body(n, u):
                need(pool, tile_lo, n + 1)
                nc.gpsimd.tensor_copy(xt_lo[:, :, ds(n * P, P)], t_lo[u][:, :, :]).then_inc(all_lo, 1)
            tiles(pool, body)

        @block.tensor
        def _(pe):
            def values(n, u):
                need(pe, tile_lo, n + 1)
                need(pe, v_copied, n - 1)
                product3(nc, ps_v[u][:, :], [(t_hi[u][:, c, :], t_lo[u][:, c, :], wv_hi[:, c, :], wv_lo[:, c, :])
                                             for c in range(KC)]).then_inc(v_done, 1)

            def body(n, u):
                need(pe, xn_ready, n + 1)
                need(pe, tile_lo, n - 1)
                need(pe, all_hi, n - 1)
                transpose_chunks(nc, ps_t[u], xn[u], ident).then_inc(transposed, 1)
                if isinstance(n, int) and n == 1:
                    pe.wait_ge(w_ready, 1)
                if exists(n - 1, TILES):
                    values(n - 1, 1 - u)
            tiles(pe, body)
            values(TILES - 1, 1)


def self_attention(nc, stack_type, x, norm2, xt_hi, xt_lo, v1, ident, wq_dram, wk_dram, wo_dram, heads_dram):
    with stack_type() as stack:
        m = Memory(nc, stack, "p3_")
        SCALE = 1.0 / float(np.sqrt(np.float32(D1)))
        ITS = G1 * NB
        SCORES, EXPS, NORMS = 3, 2, 1

        def ahead(it, j, k):
            return (it, j + k) if j + k < HPG1 else (it + 1, j + k - HPG1)
        raw = {w: m.sb(f"raw_{w}", [P, KC, P]) for w in "qk"}
        w_hi = {w: m.sb(f"w{w}_hi", [P, KC, P], F32R) for w in "qk"}
        w_lo = {w: m.sb(f"w{w}_lo", [P, KC, P], F32R) for w in "qk"}
        wo_raw = m.sb("wo_raw", [P, HIDDEN])
        wo_hi, wo_lo = m.sb("wo_hi", [P, HIDDEN], F32R), m.sb("wo_lo", [P, HIDDEN], F32R)
        heads = m.sb("heads", [P, HPG1])
        q_t, k_t = m.sb("q_t", [P, BLOCK]), m.sb("k_t", [P, BLOCK])
        q_head = m.sb("q_head", [P, HPG1, BLOCK])
        v_head = m.sb("v_head", [P, TPB, VROW])
        s = [m.sb(f"s{i}", [P, TPB, SEQ]) for i in range(2)]
        p = [m.sb(f"p{i}", [P, TPB, SEQ]) for i in range(2)]
        pd = [m.sb(f"pd{i}", [P, TPB, P]) for i in range(2)]
        pt = [m.sb(f"pt{i}", [P, BLOCK]) for i in range(2)]
        mx = [m.sb(f"mx{i}", [P, TPB]) for i in range(2)]
        total = [m.sb(f"total{i}", [P, TPB]) for i in range(2)]
        inv = [m.sb(f"inv{i}", [P, TPB]) for i in range(2)]
        o_hi, o_lo = m.sb("o_hi", [P, BLOCK], F32R), m.sb("o_lo", [P, BLOCK], F32R)
        ps_qk, ps_o = m.ps("ps_qk"), m.ps("ps_o")
        ps_s = [m.ps(f"ps_s{i}") for i in range(2)]
        ps_p = [m.ps(f"ps_p{i}") for i in range(2)]
        ps_y = [m.ps(f"ps_y{i}") for i in range(2)]
        raw_in = {w: m.sem(f"raw_in_{w}") for w in "qko"}
        part_hi = {w: m.sem(f"part_hi_{w}") for w in "qko"}
        ready = {w: m.sem(f"ready_{w}") for w in "qko"}
        heads_in, zeroed = m.sem("heads_in"), m.sem("zeroed")
        done = {"q": m.sem("q_done"), "k": m.sem("k_done")}
        q_copied, k_copied, expanded = m.sem("q_copied"), m.sem("k_copied"), m.sem("expanded")
        s_done, s_max, s_shifted = m.sem("s_done"), m.sem("s_max"), m.sem("s_shifted")
        p_exp, p_inv, p_norm, p_turned, pt_copied = (m.sem(n) for n in ("p_exp", "p_inv", "p_norm", "p_turned", "pt_copied"))
        v_ready, pv_done, out_hi, out_lo, y_done, y_added = (m.sem(n) for n in ("v_ready", "pv_done", "out_hi", "out_lo", "y_done", "y_added"))
        vh = v_head[:, :, :].rearrange("p t (j w) -> p t j w", w=VPITCH)[:, :, :, 0:D1]

        block = stack.enter_context(nc.Block())

        @block.sync
        def _(sp):
            sp.dma_start(heads[:, :], heads_dram).then_inc(heads_in, 16)

            def load(g):
                need(sp, ready["q"], g)
                sp.dma_start(raw["q"][:, :, :], wq_dram[:, :, ds(g * P, P)]).then_inc(raw_in["q"], 16)
                need(sp, ready["k"], g)
                sp.dma_start(raw["k"][:, :, :], wk_dram[:, :, ds(g * P, P)]).then_inc(raw_in["k"], 16)
                need(sp, ready["o"], g)
                sp.dma_start(wo_raw[:, :], wo_dram[ds(g * P, P), :]).then_inc(raw_in["o"], 16)
            load(0)
            with sp.Fori(1, G1) as g:
                load(g)

        def split_hi(act, w, g, after, count):
            need(act, raw_in[w], (g + 1) * 16)
            need(act, after, count)
            dst, src = (wo_hi[:, :], wo_raw[:, :]) if w == "o" else (w_hi[w][:, :, :], raw[w][:, :, :])
            nc.scalar.activation(dst, src, ACT.Copy).then_inc(part_hi[w], 1)

        def split_lo(dve, w, g):
            need(dve, part_hi[w], g + 1)
            if w == "o":
                sub = nc.vector.tensor_tensor(wo_lo[:, :], wo_raw[:, :], wo_hi[:, :], ALU.subtract)
            else:
                sub = nc.vector.tensor_tensor(w_lo[w][:, :, :], raw[w][:, :, :], w_hi[w][:, :, :], ALU.subtract)
            sub.then_inc(ready[w], 1)

        def next_group(g, b):
            return g + 1 if isinstance(b, int) and b == NB - 1 else g

        @block.tensor
        def _(pe):
            def project(w, g, it, nb, chunks=range(KC)):
                need(pe, ready[w], g + 1)
                if w == "q":
                    need(pe, k_copied, it)
                else:
                    need(pe, q_copied, it + 1)
                for c in chunks:
                    hi, lo, t_hi, t_lo = w_hi[w][:, c, :], w_lo[w][:, c, :], xt_hi[:, c, ds(nb * BLOCK, BLOCK)], xt_lo[:, c, ds(nb * BLOCK, BLOCK)]
                    nc.tensor.matmul(ps_qk[:, :], hi, t_hi, start=(c == 0), stop=False)
                    nc.tensor.matmul(ps_qk[:, :], hi, t_lo, start=False, stop=False)
                    mm = nc.tensor.matmul(ps_qk[:, :], lo, t_hi, start=False, stop=(c == KC - 1))
                if chunks[-1] == KC - 1:
                    mm.then_inc(done[w], 1)

            def scores(it, j):
                u = it * HPG1 + j
                need(pe, expanded, u + 1)
                need(pe, k_copied, it + 1)
                need(pe, s_shifted, u - 1)
                for t in range(TPB):
                    mm = nc.tensor.matmul(ps_s[j % 2][:, t * P:(t + 1) * P], q_head[:, j, t * P:(t + 1) * P],
                                          k_t[:, t * P:(t + 1) * P], start=True, stop=True)
                mm.then_inc(s_done, 1)

            def turn(it, j):
                u = it * HPG1 + j
                need(pe, p_norm, u + 1)
                need(pe, pt_copied, u - 1)
                for t in range(TPB):
                    tr = nc.tensor.transpose(ps_p[j % 2][:, t * P:(t + 1) * P], pd[j % 2][:, t, :], ident[:, :])
                tr.then_inc(p_turned, 1)

            def mix(it, j):
                u = it * HPG1 + j
                need(pe, pt_copied, u + 1)
                if j == 0:
                    need(pe, v_ready, it + 1)
                    need(pe, out_lo, it)
                for t in range(TPB):
                    mm = nc.tensor.matmul(ps_o[:, t * P:(t + 1) * P], v_head[:, t, j * P:(j + 1) * P],
                                          pt[j % 2][:, t * P:(t + 1) * P], start=(j == 0 and t == 0),
                                          stop=(j == HPG1 - 1), skip_group_check=True)
                mm.then_inc(pv_done, 1)

            def output(g, it, tiles):
                need(pe, out_lo, it + 1)
                need(pe, ready["o"], g + 1)
                for t in tiles:
                    need(pe, y_added, it * TPB + t - 1)
                    product3(nc, ps_y[t % 2][:, :], [(o_hi[:, t * P:(t + 1) * P], o_lo[:, t * P:(t + 1) * P],
                                                      wo_hi[:, :], wo_lo[:, :])]).then_inc(y_done, 1)

            def body(g, b):
                it = g * NB + b
                nb = 0 if isinstance(b, int) and b == NB - 1 else b + 1
                for j in range(HPG1):
                    if exists(ahead(it, j, SCORES)[0], ITS):
                        scores(*ahead(it, j, SCORES))
                    if exists(it + 1, ITS) and j in (1, 2):
                        project("q", next_group(g, b), it + 1, nb, (2 * j - 2, 2 * j - 1))
                    turn(it, j)
                    if exists(it + 1, ITS) and j in (3, 4):
                        project("k", next_group(g, b), it + 1, nb, (2 * j - 6, 2 * j - 5))
                    if j >= 4 and exists(it - 1, ITS):
                        output(g - 1 if isinstance(b, int) and b == 0 else g, it - 1, (j - 4,))
                    if j > 0:
                        mix(it, j - 1)
                    elif exists(it - 1, ITS):
                        mix(it - 1, HPG1 - 1)

            project("q", 0, 0, 0)
            project("k", 0, 0, 0)
            for j in range(SCORES):
                scores(0, j)
            walk(pe, G1, body)
            mix(ITS - 1, HPG1 - 1)
            output(G1 - 1, ITS - 1, range(TPB))

        @block.scalar
        def _(act):
            def copy(w, it):
                need(act, done[w], it + 1)
                if w == "q":
                    need(act, expanded, it * HPG1)
                    nc.scalar.activation(q_t[:, :], ps_qk[:, :], ACT.Copy).then_inc(q_copied, 1)
                else:
                    need(act, s_done, it * HPG1)
                    nc.scalar.activation(k_t[:, :], ps_qk[:, :], ACT.Copy).then_inc(k_copied, 1)

            def expand(it, j):
                need(act, q_copied, it + 1)
                need(act, s_done, it * HPG1 + j + 1 - HPG1)
                nc.scalar.activation(q_head[:, j, :], q_t[:, :], ACT.Copy, scale=heads[:, j:j + 1]).then_inc(expanded, 1)

            def exponentials(it, j):
                u = it * HPG1 + j
                need(act, s_shifted, u + 1)
                need(act, p_norm, u - 1)
                for t in range(TPB):
                    e = nc.scalar.activation(p[j % 2][:, t, :], s[j % 2][:, t, :], ACT.Exp, scale=SCALE,
                                             accum_out=total[j % 2][:, t:t + 1])
                e.then_inc(p_exp, 1)

            def copy_turned(it, j):
                u = it * HPG1 + j
                need(act, p_turned, u + 1)
                need(act, pv_done, u - 1)
                nc.scalar.activation(pt[j % 2][:, :], ps_p[j % 2][:, :], ACT.Copy).then_inc(pt_copied, 1)

            def outputs_hi(it):
                need(act, pv_done, (it + 1) * HPG1)
                need(act, y_done, it * TPB)
                nc.scalar.activation(o_hi[:, :], ps_o[:, :], ACT.Copy).then_inc(out_hi, 1)

            def body(g, b):
                it = g * NB + b
                last_block, first_block = (isinstance(b, int) and b == NB - 1), (isinstance(b, int) and b == 0)
                for j in range(HPG1):
                    if exists(it + 1, ITS) and last_block and j == 0:
                        split_hi(act, "q", g + 1, done["q"], it + 1)
                    if exists(it + 1, ITS) and last_block and j == 2:
                        split_hi(act, "k", g + 1, done["k"], it + 1)
                    if j == 1 and exists(it - 1, ITS):
                        outputs_hi(it - 1)
                    copy_turned(it, j)
                    if j == 4 and exists(it + 1, ITS):
                        copy("k", it + 1)
                    if exists(ahead(it, j, EXPS)[0], ITS):
                        exponentials(*ahead(it, j, EXPS))
                    if j < 2:
                        expand(it, HPG1 - 2 + j)
                    elif j > 2 and exists(it + 1, ITS):
                        expand(it + 1, j - 2)
                    if j == 2 and exists(it + 1, ITS):
                        copy("q", it + 1)
                        expand(it + 1, 0)
                    if first_block and exists(it - 1, ITS) and j == 7:
                        split_hi(act, "o", g, y_done, it * TPB)

            split_hi(act, "q", 0, done["q"], 0)
            split_hi(act, "k", 0, done["k"], 0)
            split_hi(act, "o", 0, y_done, 0)
            copy("q", 0)
            copy("k", 0)
            act.wait_ge(heads_in, 16)
            for j in range(HPG1 - 2):
                expand(0, j)
            for j in range(EXPS):
                exponentials(0, j)
            walk(act, G1, body)
            outputs_hi(ITS - 1)

        @block.vector
        def _(dve):
            def shift(it, j):
                u = it * HPG1 + j
                sc = ps_s[j % 2][:, :].rearrange("p (t k) -> p t k", t=TPB)
                need(dve, s_done, u + 1)
                for r in range(2):
                    rows = slice(r * SEQ, (r + 1) * SEQ)
                    red = nc.vector.tensor_reduce(mx[j % 2][rows, :], sc[rows, :, rows], AX.X, ALU.max)
                red.then_inc(s_max, 1)
                need(dve, s_max, u + 1)
                need(dve, p_exp, u - 1)
                for r in range(2):
                    rows = slice(r * SEQ, (r + 1) * SEQ)
                    sub = nc.vector.tensor_tensor(s[j % 2][rows, :, :], sc[rows, :, rows],
                                                  mx[j % 2][rows, :].unsqueeze(2).broadcast_to([SEQ, TPB, SEQ]), ALU.subtract)
                sub.then_inc(s_shifted, 1)

            def invert(it, j):
                need(dve, p_exp, it * HPG1 + j + 1)
                nc.vector.reciprocal(inv[j % 2][:, :], total[j % 2][:, :]).then_inc(p_inv, 1)

            def outputs_lo(it):
                need(dve, out_hi, it + 1)
                nc.vector.tensor_tensor(o_lo[:, :], ps_o[:, :], o_hi[:, :], ALU.subtract).then_inc(out_lo, 1)

            def pad_values(g, b, it):
                need(dve, pv_done, it * HPG1)
                nc.vector.tensor_copy(vh, v1[:, ds(b * TPB, TPB), ds(g * P, P)].rearrange("p t (j w) -> p t j w", w=D1)).then_inc(v_ready, 1)

            def add(g, b, it, tiles):
                for t in tiles:
                    need(dve, y_done, it * TPB + t + 1)
                    need(dve, y_added, it * TPB + t)
                    xs = x[:, ds(b * TPB + t, 1), :]
                    nc.vector.tensor_tensor(xs, ps_y[t % 2][:, :].unsqueeze(1), xs, ALU.add).then_inc(y_added, 1)
                if isinstance(g, int) and g == G1 - 1:
                    for t in tiles:
                        need(dve, y_added, it * TPB + t + 1)
                        norm2.collect(nc, b * TPB + t)

            def body(g, b):
                it = g * NB + b
                last_block, first_block = (isinstance(b, int) and b == NB - 1), (isinstance(b, int) and b == 0)
                for j in range(HPG1):
                    if exists(it + 1, ITS) and last_block and j == 0:
                        split_lo(dve, "q", g + 1)
                    if exists(it + 1, ITS) and last_block and j == 2:
                        split_lo(dve, "k", g + 1)
                    if exists(ahead(it, j, NORMS)[0], ITS):
                        invert(*ahead(it, j, NORMS))
                    if j == 1:
                        if exists(it - 1, ITS):
                            outputs_lo(it - 1)
                        pad_values(g, b, it)
                    if exists(ahead(it, j, SCORES)[0], ITS):
                        shift(*ahead(it, j, SCORES))
                    if j >= 5 and exists(it - 1, ITS):
                        add(g - 1 if first_block else g, NB - 1 if first_block else b - 1, it - 1, (j - 5,) if j < 7 else (2, 3))
                    if first_block and exists(it - 1, ITS) and j == 7:
                        split_lo(dve, "o", g)

            for w in "qko":
                split_lo(dve, w, 0)
            dve.wait_ge(zeroed, 3)
            for j in range(SCORES):
                shift(0, j)
            invert(0, 0)
            walk(dve, G1, body)
            outputs_lo(ITS - 1)
            add(G1 - 1, NB - 1, ITS - 1, range(TPB))

        @block.gpsimd
        def _(pool):
            def normalise_p(it, j):
                u = it * HPG1 + j
                need(pool, p_inv, u + 1)
                need(pool, p_turned, u - 1)
                for r in range(2):
                    rows = slice(r * SEQ, (r + 1) * SEQ)
                    mul = nc.gpsimd.tensor_tensor(pd[j % 2][rows, :, rows], p[j % 2][rows, :, :],
                                                  inv[j % 2][rows, :].unsqueeze(2).broadcast_to([SEQ, TPB, SEQ]), ALU.mult)
                mul.then_inc(p_norm, 1)

            def body(g, b):
                it = g * NB + b
                for j in range(HPG1):
                    if exists(ahead(it, j, NORMS)[0], ITS):
                        normalise_p(*ahead(it, j, NORMS))

            for buffer in (*pd, v_head):
                nc.gpsimd.memset(buffer[:, :, :], 0.0).then_inc(zeroed, 1)
            pool.wait_ge(zeroed, 3)
            normalise_p(0, 0)
            walk(pool, G1, body)


def rotate_terms(nc, ps, cos, sin, a, b):
    nc.vector.tensor_tensor(a[:, :], ps[:, :], cos, ALU.mult)
    nc.vector.tensor_tensor(b[0:HALF, :], ps[HALF:D2, :], sin[HALF:D2], ALU.mult)
    return nc.vector.tensor_tensor(b[HALF:D2, :], ps[0:HALF, :], sin[0:HALF], ALU.mult)


def keys_and_values(nc, stack_type, x, norm1, ident, x_dram, ident_dram, pos_dram, table_dram, ctx_dram, wk_dram, wv_dram,
                    k_scr, v_scr, cos_scr, sin_scr):
    with stack_type() as stack:
        m = Memory(nc, stack, "p1_")
        NKV = KVH * D2
        NH = NKV // BLOCK
        cos_t, sin_t = m.sb("cos_t", [P, TOKENS]), m.sb("sin_t", [P, TOKENS])
        pos = m.sb("pos", [P, TILES], mybir.dt.uint32)
        rows = m.sb("rows", [P, TILES, 2 * D2])
        raw = {w: m.sb(f"raw_{w}", [P, KC, NKV]) for w in "kv"}
        w_hi = {w: m.sb(f"w{w}_hi", [P, KC, NKV], F32R) for w in "kv"}
        w_lo = {w: m.sb(f"w{w}_lo", [P, KC, NKV], F32R) for w in "kv"}
        c_raw = [raw["k"][:, :, 0:BLOCK]] + [raw["v"][:, :, 0:BLOCK]] * (NB - 1)
        c_hi, c_lo = ([m.sb(f"c_{part}{i}", [P, KC, BLOCK], F32R) for i in range(2)] for part in ("hi", "lo"))
        ra, rb = m.sb("ra", [P, BLOCK]), m.sb("rb", [P, BLOCK])
        k_out = [m.sb(f"k_out{i}", [P, BLOCK]) for i in range(2)]
        v_out = [m.sb(f"v_out{i}", [P, BLOCK]) for i in range(2)]
        ps_r = [m.ps(f"ps_r{i}") for i in range(2)]
        ps_k = [m.ps(f"ps_k{i}") for i in range(2)]
        ps_v = [m.ps(f"ps_v{i}") for i in range(2)]
        pos_in, id_in, row_in, row_turned, row_copied, tables_out = (
            m.sem(n) for n in ("pos_in", "id_in", "row_in", "row_turned", "row_copied", "tables_out"))
        x_in = [m.sem(f"x_in{h}") for h in range(2)]
        k_raw_in = [m.sem(f"k_raw_in{i}") for i in range(KVH // 2)]
        v_raw_in = [m.sem(f"v_raw_in{i}") for i in range(NH * KC)]
        c_in0 = [m.sem(f"c_in0_{c}") for c in range(KC)]
        c_in = m.sem("c_in")
        part_hi, ready = {w: m.sem(f"part_hi_{w}") for w in "kv"}, {w: m.sem(f"ready_{w}") for w in "kv"}
        c_part, c_ready = m.sem("c_part"), m.sem("c_ready")
        k_done, v_done, k_terms, k_added, v_copied = (m.sem(n) for n in ("k_done", "v_done", "k_terms", "k_added", "v_copied"))
        k_stored, v_stored = [m.sem(f"k_stored{i}") for i in range(2)], [m.sem(f"v_stored{i}") for i in range(2)]
        block = stack.enter_context(nc.Block())

        def blocks(first, body):
            first()
            for b in range(1, NB):
                body(b)

        @block.sync
        def _(sp):
            for c in range(KC):
                sp.dma_start(c_raw[0][:, c, :], ctx_dram[:, c, 0:BLOCK]).then_inc(c_in0[c], 16)
                sp.dma_start(raw["v"][:, c, 0:BLOCK], wv_dram[:, c, 0:BLOCK]).then_inc(v_raw_in[c], 16)
            sp.dma_start(ident[:, :], ident_dram).then_inc(id_in, 16)
            for c in range(KC):
                sp.dma_start(raw["v"][:, c, BLOCK:NKV], wv_dram[:, c, BLOCK:NKV]).then_inc(v_raw_in[KC + c], 16)
            sp.wait_ge(c_ready, KC)
            for i in range(KVH):
                sp.dma_start(raw["k"][:, :, i * D2:(i + 1) * D2], wk_dram[:, :, i * D2:(i + 1) * D2]).then_inc(k_raw_in[i // 2], 16)

            def load_tokens(t):
                sp.dma_start(x[:, t, :], x_dram[:, t, :]).then_inc(x_in[t // KVH], 16)

            def store_tables(i):
                out, table = ((cos_scr, cos_t), (sin_scr, sin_t))[i % 2]
                cols = slice(i // 2 * BLOCK, (i // 2 + 1) * BLOCK)
                sp.dma_start(out[:, cols], table[:, cols]).then_inc(tables_out, 16)

            def store_keys(b, i):
                need(sp, k_added, b * KVH + i + 1)
                sp.dma_start(k_scr[i, ds(b, 1), :, :].rearrange("b p n -> p (b n)"), k_out[i % 2][:, :]).then_inc(k_stored[i % 2], 16)

            def store_values(b, i):
                need(sp, v_copied, b * KVH + i + 1)
                t, g0 = i % TPB, (i // TPB) * (KVH // NH)
                sp.dma_start(v_scr[g0:g0 + KVH // NH, ds(b, 1), :, t, :].rearrange("g b p d -> p (g b) d"),
                             v_out[i % 2][:, :].rearrange("p (g d) -> p g d", d=D2)).then_inc(v_stored[i % 2], 16)

            def first():
                for i in range(KVH):
                    store_values(0, i)
                load_context(1)
                sp.wait_ge(row_copied, 2 * NB)
                for i in range(KVH):
                    store_keys(0, i)
                    load_tokens(i)

            def load_context(b):
                need(sp, c_ready, b * KC)
                sp.wait_ge(ready["v"], NH * KC)
                sp.dma_start(c_raw[b], ctx_dram[:, :, ds(b * BLOCK, BLOCK)]).then_inc(c_in, 16)

            def body(b):
                if b + 1 < NB:
                    load_context(b + 1)
                for i in range(KVH):
                    store_keys(b, i)
                    store_values(b, i)
                    if b == 1:
                        load_tokens(KVH + i)
                    if b == 2:
                        store_tables(i)
            blocks(first, body)
            sp.wait_ge(tables_out, 16 * 2 * NB)
            for i in range(2):
                sp.wait_ge(k_stored[i], 16 * NB * KVH // 2)
                sp.wait_ge(v_stored[i], 16 * NB * KVH // 2)

        @block.gpsimd
        def _(pool):
            pool.dma_start(pos[:, :], pos_dram).then_inc(pos_in, 16)
            pool.wait_ge(pos_in, 16)
            for t in range(TILES):
                pool.indirect_dma_start(rows[:, t, :], None, table_dram, bass.IndirectOffsetOnAxis(ap=pos[:, t:t + 1], axis=0)).then_inc(row_in, 16)

            def body(b):
                for i in range(KVH):
                    n = b * KVH + i
                    need(pool, k_terms, n + 1)
                    need(pool, k_stored[i % 2], (b * (KVH // 2) + i // 2) * 16)
                    nc.gpsimd.tensor_tensor(k_out[i % 2][:, :], ra[:, :], rb[:, :], ALU.add).then_inc(k_added, 1)
            blocks(lambda: body(0), body)

        @block.scalar
        def _(act):
            def context_hi(b, c):
                nc.scalar.activation(c_hi[b % 2][:, c, :], c_raw[b][:, c, :], ACT.Copy).then_inc(c_part, 1)

            def value_weights_hi(n):
                h, c = n // KC, n % KC
                act.wait_ge(v_raw_in[n], 16)
                cols = slice(h * BLOCK, (h + 1) * BLOCK)
                nc.scalar.activation(w_hi["v"][:, c, cols], raw["v"][:, c, cols], ACT.Copy).then_inc(part_hi["v"], 1)

            def key_weights_hi(i):
                act.wait_ge(k_raw_in[i // 2], 32)
                cols = slice(i * D2, (i + 1) * D2)
                nc.scalar.activation(w_hi["k"][:, :, cols], raw["k"][:, :, cols], ACT.Copy).then_inc(part_hi["k"], 1)

            def copy_values(b, i):
                need(act, v_done, b * KVH + i + 1)
                need(act, v_stored[i % 2], (b * (KVH // 2) + i // 2) * 16)
                nc.scalar.activation(v_out[i % 2][:, :], ps_v[i % 2][:, :], ACT.Copy).then_inc(v_copied, 1)

            def first():
                for c in range(KC):
                    act.wait_ge(c_in0[c], 16)
                    context_hi(0, c)
                    value_weights_hi(c)
                for c in range(KC):
                    value_weights_hi(KC + c)
                for i in range(KVH):
                    copy_values(0, i)
                    key_weights_hi(i)
                for n in range(2 * NB):
                    act.wait_ge(row_turned, n + 1)
                    dst = (cos_t, sin_t)[n % 2]
                    nc.scalar.activation(dst[:, (n // 2) * BLOCK:(n // 2 + 1) * BLOCK], ps_r[n % 2][:, :], ACT.Copy).then_inc(row_copied, 1)
                act.wait_ge(c_in, 16)
                for c in range(KC):
                    context_hi(1, c)

            def body(b):
                for i in range(KVH):
                    copy_values(b, i)
                    if b + 1 < NB and i == 1:
                        need(act, c_in, (b + 1) * 16)
                        need(act, k_done, b * KVH)
                        need(act, v_done, b * KVH)
                    if b + 1 < NB and i % 2 == 1:
                        context_hi(b + 1, i // 2)
            blocks(first, body)

        @block.vector
        def _(dve):
            def context_lo(b, c):
                need(dve, c_part, b * KC + c + 1)
                nc.vector.tensor_tensor(c_lo[b % 2][:, c, :], c_raw[b][:, c, :], c_hi[b % 2][:, c, :], ALU.subtract).then_inc(c_ready, 1)

            def value_weights_lo(n):
                h, c = n // KC, n % KC
                dve.wait_ge(part_hi["v"], n + 1)
                cols = slice(h * BLOCK, (h + 1) * BLOCK)
                nc.vector.tensor_tensor(w_lo["v"][:, c, cols], raw["v"][:, c, cols], w_hi["v"][:, c, cols], ALU.subtract).then_inc(ready["v"], 1)

            def key_weights_lo(i):
                dve.wait_ge(part_hi["k"], i + 1)
                cols = slice(i * D2, (i + 1) * D2)
                nc.vector.tensor_tensor(w_lo["k"][:, :, cols], raw["k"][:, :, cols], w_hi["k"][:, :, cols], ALU.subtract).then_inc(ready["k"], 1)

            def rotate(b, i):
                n = b * KVH + i
                need(dve, k_done, n + 1)
                need(dve, k_added, n)
                rotate_terms(nc, ps_k[i % 2], cos_t[:, ds(b * BLOCK, BLOCK)], sin_t[:, ds(b * BLOCK, BLOCK)], ra, rb).then_inc(k_terms, 1)

            def first():
                for c in range(KC):
                    context_lo(0, c)
                    value_weights_lo(c)
                for c in range(KC):
                    value_weights_lo(KC + c)
                for i in range(KVH):
                    key_weights_lo(i)
                dve.wait_ge(row_copied, 2 * NB)
                for i in range(KVH):
                    rotate(0, i)
                    if i < KC:
                        context_lo(1, i)

            def body(b):
                for i in range(KVH):
                    rotate(b, i)
                    if b + 1 < NB and i % 2 == 1:
                        context_lo(b + 1, i // 2)
                    if b < 3:
                        t = (b - 1) * KVH + i
                        if t % KVH == 0:
                            dve.wait_ge(x_in[t // KVH], 16 * KVH)
                        norm1.collect(nc, t)
            blocks(first, body)

        @block.tensor
        def _(pe):
            def keys(b, i, before=lambda c: None):
                need(pe, k_terms, b * KVH + i - 1)
                cols = slice(i * D2, (i + 1) * D2)
                product3(nc, ps_k[i % 2][:, :], [(w_hi["k"][:, c, cols], w_lo["k"][:, c, cols], c_hi[b % 2][:, c, :], c_lo[b % 2][:, c, :])
                                                 for c in range(KC)], before).then_inc(k_done, 1)

            def values(b, i, before=lambda c: None):
                need(pe, v_copied, b * KVH + i - 1)
                t, h = i % TPB, i // TPB
                tile, cols = slice(t * P, (t + 1) * P), slice(h * BLOCK, (h + 1) * BLOCK)
                product3(nc, ps_v[i % 2][:, :], [(c_hi[b % 2][:, c, tile], c_lo[b % 2][:, c, tile], w_hi["v"][:, c, cols], w_lo["v"][:, c, cols])
                                                 for c in range(KC)], before).then_inc(v_done, 1)

            def weights_and_context(c):
                pe.wait_ge(c_ready, c + 1)
                pe.wait_ge(ready["v"], c + 1)

            def first():
                values(0, 0, weights_and_context)
                for i in range(1, KVH):
                    if i == TPB:
                        pe.wait_ge(ready["v"], NH * KC)
                    values(0, i)
                pe.wait_ge(id_in, 16)
                pe.wait_ge(row_in, 16 * TILES)
                for n in range(2 * NB):
                    blk, part = n // 2, n % 2
                    need(pe, row_copied, n - 1)
                    for t in range(TPB):
                        tr = nc.tensor.transpose(ps_r[part][:, t * P:(t + 1) * P], rows[:, blk * TPB + t, part * D2:(part + 1) * D2], ident[:, :])
                    tr.then_inc(row_turned, 1)
                for i in range(KVH):
                    pe.wait_ge(ready["k"], i + 1)
                    keys(0, i)

            def body(b):
                for i in range(KVH):
                    keys(b, i, (lambda c: need(pe, c_ready, b * KC + c + 1)) if i == 0 else (lambda c: None))
                    values(b, i)
            blocks(first, body)


def cross_attention(nc, stack_type, x, norm2, norm3, xt_hi, xt_lo, cos_t, sin_t, bound, ident, mask_dram, cos_scr, sin_scr,
                    wq_dram, wo_dram, k_scr, v_scr):
    with stack_type() as stack:
        m = Memory(nc, stack, "p4_")
        SCALE = 1.0 / float(np.sqrt(np.float32(D2)))
        ITS, H = KVH * NB, HPG2
        UNITS, PAIR, UT = 4, 2, TPB // 2
        UB = UT * P // SEQ
        QUERIES = 3
        raw = {w: [m.sb(f"raw_{w}{i}", [P, HIDDEN]) for i in range(2)] for w in "qo"}
        w_hi = {w: [m.sb(f"w{w}_hi{h}", [P, HIDDEN], F32R) for h in range(H)] for w in "qo"}
        w_lo = {w: [m.sb(f"w{w}_lo{h}", [P, HIDDEN], F32R) for h in range(H)] for w in "qo"}
        k_t = m.sb("k_t", [P, 2, BLOCK + SEQ])
        v_in = m.sb("v_in", [P, BLOCK])
        v_hi, v_lo = m.sb("v_hi", [P, BLOCK], F32R), m.sb("v_lo", [P, BLOCK], F32R)
        q_rot = m.sb("q_rot", [P, H // PAIR, BLOCK // SEQ, PAIR, SEQ])
        ra, rb = m.sb("ra", [P, BLOCK]), m.sb("rb", [P, BLOCK])
        s = [m.sb(f"s{i}", [P, UB, SEQ]) for i in range(2)]
        p_both, pn_both = m.sb("p", [P, 2, UB, SEQ]), m.sb("pn", [P, 2, UB, SEQ])
        p, pn = ([both[:, i, :, :] for i in range(2)] for both in (p_both, pn_both))
        xn = [both[:, :, :, :].rearrange("p i b k -> p (i b k)") for both in (p_both, pn_both)]
        pt_hi = [m.sb(f"pt_hi{i}", [P, UT, PAIR, 2, SEQ], F32R) for i in range(2)]
        pt_lo = [m.sb(f"pt_lo{i}", [P, UT, PAIR, 2, SEQ], F32R) for i in range(2)]
        mx = [m.sb(f"mx{i}", [P, UB]) for i in range(2)]
        shift_by = [m.sb(f"shift{i}", [P, UB]) for i in range(2)]
        total = [m.sb(f"total{i}", [P, UB]) for i in range(2)]
        inv = [m.sb(f"inv{i}", [P, UB]) for i in range(2)]
        o_hi = [m.sb(f"o_hi{i}", [P, UT, PAIR, P], F32R) for i in range(2)]
        o_lo = [m.sb(f"o_lo{i}", [P, UT, PAIR, P], F32R) for i in range(2)]
        ps_q, ps_s, ps_p, ps_o = m.ps("ps_q"), m.ps("ps_s"), m.ps("ps_p"), m.ps("ps_o")
        ps_y = [m.ps(f"ps_y{t}") for t in range(TPB)]
        ps_t = ps_y[2:4]
        mask_in, masked, tables_in = m.sem("mask_in"), m.sem("masked"), m.sem("tables_in")
        xn_ready, transposed, all_hi, all_lo = (m.sem(n) for n in ("xn_ready", "transposed", "all_hi", "all_lo"))
        raw_in = {w: [m.sem(f"raw_in_{w}{i}") for i in range(2)] for w in "qo"}
        part_hi, ready = {w: m.sem(f"part_hi_{w}") for w in "qo"}, {w: m.sem(f"ready_{w}") for w in "qo"}
        k_in, v_loaded, v_part, v_ready, zeroed = (m.sem(n) for n in ("k_in", "v_loaded", "v_part", "v_ready", "zeroed"))
        q_done, q_terms, q_added = m.sem("q_done"), m.sem("q_terms"), m.sem("q_added")
        s_done, s_bound, s_max, s_shift = m.sem("s_done"), m.sem("s_bound"), m.sem("s_max"), m.sem("s_shift")
        p_exp, p_inv, p_norm, p_turned = (m.sem(n) for n in ("p_exp", "p_inv", "p_norm", "p_turned"))
        pt_part, pt_ready = m.sem("pt_part"), m.sem("pt_ready")
        pv_done, out_hi, out_lo, y_done, y_added = (m.sem(n) for n in ("pv_done", "out_hi", "out_lo", "y_done", "y_added"))
        block = stack.enter_context(nc.Block())

        def is_last(b):
            return isinstance(b, int) and b == NB - 1

        def is_first(b):
            return isinstance(b, int) and b == 0

        def ahead(g, b, i, k):
            if i + k < UNITS:
                return g, b, g * NB + b, i + k
            if is_last(b):
                return g + 1, 0, (g + 1) * NB, i + k - UNITS
            return g, b + 1, g * NB + b + 1, i + k - UNITS

        def turned(rows):
            return ps_p[rows, 0:UT * P].rearrange("p (t h q) -> p t h q", t=UT, h=PAIR)

        @block.sync
        def _(sp):
            def load(w, g, h):
                need(sp, ready[w], 4 * g + h - 1)
                if w == "q":
                    sp.dma_start(raw["q"][h % 2][:, :].rearrange("p (c d) -> p c d", c=KC),
                                 wq_dram[:, :, ds((g * H + h) * D2, D2)]).then_inc(raw_in["q"][h % 2], 16)
                else:
                    sp.dma_start(raw["o"][h % 2][:, :], wo_dram[ds((g * H + h) * D2, D2), :]).then_inc(raw_in["o"][h % 2], 16)

            load("q", 0, 0)
            load("q", 0, 1)
            sp.dma_start(cos_t[:, :], cos_scr).then_inc(tables_in, 16)
            sp.dma_start(sin_t[:, :], sin_scr).then_inc(tables_in, 16)
            load("q", 0, 2)
            load("q", 0, 3)
            for r in range(2):
                sp.dma_start(bound[r * SEQ:(r + 1) * SEQ, :, :].bitcast(I32), mask_dram).then_inc(mask_in, 16)
            for h in range(H):
                load("o", 0, h)
            with sp.Fori(1, KVH) as g:
                for w in "qo":
                    for h in range(H):
                        load(w, g, h)

        def split_hi(act, w, g, h, after, count):
            need(act, raw_in[w][h % 2], (2 * g + h // 2 + 1) * 16)
            need(act, after, count)
            nc.scalar.activation(w_hi[w][h][:, :], raw[w][h % 2][:, :], ACT.Copy).then_inc(part_hi[w], 1)

        def split_lo(pool, w, g, h):
            need(pool, part_hi[w], 4 * g + h + 1)
            nc.gpsimd.tensor_tensor(w_lo[w][h][:, :], raw[w][h % 2][:, :], w_hi[w][h][:, :], ALU.subtract).then_inc(ready[w], 1)

        def renewed_q(g, b, i):
            if is_last(b) and exists(g + 1, KVH):
                return [("q", g + 1, i, q_done, (g * NB + b) * UNITS + i + 1)]
            return []

        def renewed_o(g, b, i):
            n = (g * NB + b) * UNITS + i
            if is_last(b) and i >= 2 and exists(g + 1, KVH):
                return [("o", g + 1, i - 2, y_done, (n - i + 2) * UT)]
            if is_first(b) and i < 2 and not (isinstance(g, int) and g == 0):
                return [("o", g, i + 2, y_done, (n - i) * UT)]
            return []

        @block.tensor
        def _(pe):
            def queries(g, b, it, h, before=lambda c: None):
                need(pe, ready["q"], 4 * g + h + 1)
                need(pe, q_terms, it * H + h)
                product3(nc, ps_q[:, :], [(w_hi["q"][h][:, c * P:(c + 1) * P], w_lo["q"][h][:, c * P:(c + 1) * P],
                                           xt_hi[:, c, ds(b * BLOCK, BLOCK)], xt_lo[:, c, ds(b * BLOCK, BLOCK)])
                                          for c in range(KC)], before).then_inc(q_done, 1)

            def scores(g, b, it, i):
                pair, first = i // 2, i % 2 * UB
                need(pe, q_added, it * H + pair * PAIR + PAIR)
                need(pe, k_in, (it + 1) * 16)
                need(pe, s_bound, it * UNITS + i)
                for j in range(UB):
                    start = (first + j) * SEQ
                    mm = nc.tensor.matmul(ps_s[:, j * P:(j + 1) * P], q_rot[:, pair, first + j, :, :].rearrange("p h q -> p (h q)"),
                                          k_t[:, ds(it % 2, 1), start:start + P].squeeze(1), start=True, stop=True)
                mm.then_inc(s_done, 1)

            def turn(it, i):
                n = it * UNITS + i
                need(pe, p_norm, n + 1)
                need(pe, pt_ready, n)
                for t in range(UT):
                    tr = nc.tensor.transpose(ps_p[:, t * P:(t + 1) * P], pn[i % 2][:, 2 * t:2 * t + 2, :].rearrange("p b k -> p (b k)"),
                                             ident[:, :])
                tr.then_inc(p_turned, 1)

            def mix(it, i):
                n = it * UNITS + i
                if i == 0:
                    need(pe, v_ready, it + 1)
                need(pe, pt_ready, n + 1)
                need(pe, out_lo, n)
                for t in range(UT):
                    tile = slice((i % 2 * UT + t) * P, (i % 2 * UT + t + 1) * P)
                    mm = product3(nc, ps_o[:, t * 2 * P:(t + 1) * 2 * P],
                                  [(v_hi[:, tile], v_lo[:, tile], pt_hi[i % 2][:, t, :, :, :].rearrange("p h b q -> p (h b q)"),
                                    pt_lo[i % 2][:, t, :, :, :].rearrange("p h b q -> p (h b q)"))])
                mm.then_inc(pv_done, 1)

            def output(g, it, i):
                n, first = it * UNITS + i, i // 2 * PAIR
                need(pe, out_lo, n + 1)
                need(pe, ready["o"], 4 * g + first + PAIR)
                for t in range(UT):
                    tile = i % 2 * UT + t
                    if first == 0:
                        need(pe, y_added, (it - 1) * TPB + tile + 1)
                    for j in range(PAIR):
                        h = first + j
                        oh, ol = o_hi[i % 2][:, t, j, :], o_lo[i % 2][:, t, j, :]
                        nc.tensor.matmul(ps_y[tile][:, :], oh, w_hi["o"][h][:, :], start=(h == 0), stop=False)
                        nc.tensor.matmul(ps_y[tile][:, :], oh, w_lo["o"][h][:, :], start=False, stop=False)
                        mm = nc.tensor.matmul(ps_y[tile][:, :], ol, w_hi["o"][h][:, :], start=False, stop=(h == H - 1))
                    mm.then_inc(y_done, 1)

            def body(g, b):
                it = g * NB + b
                for i in range(UNITS):
                    gq, bq, itq, hq = ahead(g, b, i, QUERIES)
                    if exists(itq, ITS):
                        queries(gq, bq, itq, hq)
                    g1, b1, it1, i1 = ahead(g, b, i, 1)
                    if exists(it1, ITS):
                        scores(g1, b1, it1, i1)
                    turn(it, i)
                    if i > 0:
                        output(g, it, i - 1)
                    elif exists(it - 1, ITS):
                        output(g - 1 if is_first(b) else g, it - 1, UNITS - 1)
                    mix(it, i)

            def turn_tile(t):
                need(pe, xn_ready, t + 1)
                need(pe, all_lo, t - 1)
                transpose_chunks(nc, ps_t[t % 2], xn[t % 2], ident).then_inc(transposed, 1)

            for t in range(TPB):
                turn_tile(t)
            for h in range(QUERIES):
                need(pe, all_lo, TPB)
                queries(0, 0, 0, h, lambda c: turn_tile((h + 1) * TPB + c))
            pe.wait_ge(zeroed, 5)
            scores(0, 0, 0, 0)
            need(pe, all_lo, TILES)
            walk(pe, KVH, body)
            output(KVH - 1, ITS - 1, UNITS - 1)

        @block.scalar
        def _(act):
            def load_kv(g, b, it):
                need(act, k_in, it * 16)
                need(act, s_done, (it - 1) * UNITS)
                act.dma_start(k_t[:, ds(it % 2, 1), 0:BLOCK], k_scr[ds(g, 1), ds(b, 1), :, :].rearrange("g b p n -> p (g b) n")).then_inc(k_in, 16)
                need(act, v_loaded, it * 16)
                need(act, v_ready, it)
                act.dma_start(v_in[:, :].unsqueeze(1), v_scr[ds(g, 1), ds(b, 1), :, :, :].rearrange("g b p t d -> p (g b) (t d)")).then_inc(v_loaded, 16)

            def values_hi(it):
                need(act, v_loaded, (it + 1) * 16)
                need(act, pv_done, it * UNITS)
                nc.scalar.activation(v_hi[:, :], v_in[:, :], ACT.Copy).then_inc(v_part, 1)

            def exponentials(it, i):
                n = it * UNITS + i
                need(act, s_shift, n + 1)
                need(act, p_norm, n - 1)
                for j in range(UB):
                    e = nc.scalar.activation(p[i % 2][:, j, :], s[i % 2][:, j, :], ACT.Exp, bias=shift_by[i % 2][:, j:j + 1],
                                             scale=SCALE, accum_out=total[i % 2][:, j:j + 1])
                e.then_inc(p_exp, 1)

            def turned_hi(it, i):
                n = it * UNITS + i
                need(act, p_turned, n + 1)
                need(act, pv_done, n - 1)
                for r in range(2):
                    rows = slice(r * SEQ, (r + 1) * SEQ)
                    c = nc.scalar.activation(pt_hi[i % 2][rows, :, :, r, :], turned(rows), ACT.Copy)
                c.then_inc(pt_part, 1)

            def outputs_hi(it, i):
                n = it * UNITS + i
                need(act, pv_done, n + 1)
                need(act, y_done, (n - 1) * UT)
                nc.scalar.activation(o_hi[i % 2].rearrange("p t h n -> p (t h n)"), ps_o[:, :], ACT.Copy).then_inc(out_hi, 1)

            def body(g, b):
                it = g * NB + b
                for i in range(UNITS):
                    if i > 0:
                        outputs_hi(it, i - 1)
                    else:
                        if exists(it - 1, ITS):
                            outputs_hi(it - 1, UNITS - 1)
                        values_hi(it)
                    for w, gw, hw, after, count in renewed_q(g, b, i):
                        split_hi(act, w, gw, hw, after, count)
                    turned_hi(it, i)
                    for w, gw, hw, after, count in renewed_o(g, b, i):
                        split_hi(act, w, gw, hw, after, count)
                    if i == 1 and exists(it + 1, ITS):
                        load_kv(*ahead(g, b, UNITS - 1, 1)[:3])
                    _, _, it1, i1 = ahead(g, b, i, 1)
                    if exists(it1, ITS):
                        exponentials(it1, i1)

            load_kv(0, 0, 0)
            norm2.finish_scalar(nc, act)
            for b, weights in enumerate((("q0", "q1"), (), ("q2", "q3"), ("o0", "o1"))):
                for w, h in weights:
                    split_hi(act, w, 0, int(h), q_done, 0)
                for t in range(b * TPB, (b + 1) * TPB):
                    need(act, transposed, t + 1)
                    nc.scalar.activation(xt_hi[:, :, t * P:(t + 1) * P], ps_t[t % 2][:, :].rearrange("p (c n) -> p c n", c=KC),
                                         ACT.Copy).then_inc(all_hi, 1)
            for h in range(2, H):
                split_hi(act, "o", 0, h, y_done, 0)
            exponentials(0, 0)
            act.wait_ge(zeroed, 5)
            walk(act, KVH, body)
            outputs_hi(ITS - 1, UNITS - 1)

        @block.vector
        def _(dve):
            def maxima(b, it, i):
                n = it * UNITS + i
                sc = ps_s[:, :].rearrange("p (j k) -> p j k", j=UB)
                need(dve, s_done, n + 1)
                need(dve, p_exp, n - 1)
                nc.vector.tensor_tensor(s[i % 2][:, :, :], sc[:, :, 0:SEQ], bound[:, ds(b * (BLOCK // SEQ) + i % 2 * UB, UB), :],
                                        ALU.min).then_inc(s_bound, 1)
                need(dve, s_bound, n + 1)
                nc.vector.tensor_reduce(mx[i % 2][:, :], s[i % 2][:, :, :], AX.X, ALU.max).then_inc(s_max, 1)
                need(dve, s_max, n + 1)
                nc.vector.tensor_scalar(shift_by[i % 2][:, :], mx[i % 2][:, :], -SCALE, None, ALU.mult).then_inc(s_shift, 1)

            def invert(it, i):
                need(dve, p_exp, it * UNITS + i + 1)
                nc.vector.reciprocal(inv[i % 2][:, :], total[i % 2][:, :]).then_inc(p_inv, 1)

            def rotate(b, it, h):
                m = it * H + h
                need(dve, q_done, m + 1)
                need(dve, q_added, m)
                rotate_terms(nc, ps_q, cos_t[:, ds(b * BLOCK, BLOCK)], sin_t[:, ds(b * BLOCK, BLOCK)], ra, rb).then_inc(q_terms, 1)

            def turned_lo(it, i):
                need(dve, pt_part, it * UNITS + i + 1)
                for r in range(2):
                    rows = slice(r * SEQ, (r + 1) * SEQ)
                    d = nc.vector.tensor_tensor(pt_lo[i % 2][rows, :, :, r, :], turned(rows),
                                                pt_hi[i % 2][rows, :, :, r, :], ALU.subtract)
                d.then_inc(pt_ready, 1)

            def outputs_lo(it, i):
                need(dve, out_hi, it * UNITS + i + 1)
                nc.vector.tensor_tensor(o_lo[i % 2].rearrange("p t h n -> p (t h n)"), ps_o[:, :],
                                        o_hi[i % 2].rearrange("p t h n -> p (t h n)"), ALU.subtract).then_inc(out_lo, 1)

            def add(g, b, it, tile):
                need(dve, y_done, (it * UNITS + 2) * UT + tile + 1)
                need(dve, y_added, it * TPB + tile)
                xs = x[:, ds(b * TPB + tile, 1), :]
                nc.vector.tensor_tensor(xs, ps_y[tile][:, :].unsqueeze(1), xs, ALU.add).then_inc(y_added, 1)
                if isinstance(g, int) and g == KVH - 1:
                    need(dve, y_added, it * TPB + tile + 1)
                    norm3.collect(nc, b * TPB + tile)

            def body(g, b):
                it = g * NB + b
                before = (g - 1 if is_first(b) else g, NB - 1 if is_first(b) else b - 1, it - 1)
                for i in range(UNITS):
                    if i > 0:
                        outputs_lo(it, i - 1)
                    elif exists(it - 1, ITS):
                        outputs_lo(it - 1, UNITS - 1)
                    invert(it, i)
                    if i < 2 and exists(it - 1, ITS):
                        add(*before, i * UT)
                    _, bq, itq, hq = ahead(g, b, i, QUERIES)
                    if exists(itq, ITS):
                        rotate(bq, itq, hq)
                    turned_lo(it, i)
                    _, b1, it1, i1 = ahead(g, b, i, 1)
                    if exists(it1, ITS):
                        maxima(b1, it1, i1)
                    if i < 2 and exists(it - 1, ITS):
                        add(*before, i * UT + 1)

            def norm(t):
                need(dve, transposed, t - 1)
                norm2.apply(nc, xn[t % 2], t).then_inc(xn_ready, 1)

            norm2.finish_vector(nc, dve)
            norm(0)
            for b in range(NB):
                for t in range(b * TPB, (b + 1) * TPB):
                    if t + 1 < TILES:
                        norm(t + 1)
                    need(dve, all_hi, t + 1)
                    nc.vector.tensor_tensor(xt_lo[:, :, t * P:(t + 1) * P], ps_t[t % 2][:, :].rearrange("p (c n) -> p c n", c=KC),
                                            xt_hi[:, :, t * P:(t + 1) * P], ALU.subtract).then_inc(all_lo, 1)
                if b == 0:
                    dve.wait_ge(tables_in, 32)
                else:
                    rotate(0, 0, b - 1)
                if b == 2:
                    dve.wait_ge(mask_in, 32)
                    nc.vector.tensor_scalar(bound[:, :, :], bound[:, :, :].bitcast(I32), 0, OPEN, ALU.not_equal, ALU.mult).then_inc(masked, 1)
                    dve.wait_ge(masked, 1)
                    nc.vector.tensor_scalar(bound[:, :, :], bound[:, :, :], MASKED, None, ALU.add).then_inc(masked, 1)
            dve.wait_ge(masked, 2)
            maxima(0, 0, 0)
            dve.wait_ge(zeroed, 5)
            walk(dve, KVH, body)
            outputs_lo(ITS - 1, UNITS - 1)
            for tile in range(TPB):
                add(KVH - 1, NB - 1, ITS - 1, tile)

        @block.gpsimd
        def _(pool):
            def normalise_p(it, i):
                n = it * UNITS + i
                need(pool, p_inv, n + 1)
                need(pool, p_turned, n - 1)
                nc.gpsimd.tensor_tensor(pn[i % 2][:, :, :], p[i % 2][:, :, :], inv[i % 2][:, :].unsqueeze(2).broadcast_to([P, UB, SEQ]),
                                        ALU.mult).then_inc(p_norm, 1)

            def add_terms(it, h):
                need(pool, q_terms, it * H + h + 1)
                need(pool, s_done, (it - 1) * UNITS + h // 2 * 2 + 2)
                nc.gpsimd.tensor_tensor(q_rot[:, h // PAIR, :, h % PAIR, :], ra[:, :].rearrange("p (b q) -> p b q", q=SEQ),
                                        rb[:, :].rearrange("p (b q) -> p b q", q=SEQ), ALU.add).then_inc(q_added, 1)

            def values_lo(it):
                need(pool, v_part, it + 1)
                nc.gpsimd.tensor_tensor(v_lo[:, :], v_in[:, :], v_hi[:, :], ALU.subtract).then_inc(v_ready, 1)

            def body(g, b):
                it = g * NB + b
                for i in range(UNITS):
                    normalise_p(it, i)
                    if i == 0:
                        values_lo(it)
                    for w, gw, hw, _, _ in renewed_q(g, b, i):
                        split_lo(pool, w, gw, hw)
                    _, _, itq, hq = ahead(g, b, i, QUERIES)
                    if exists(itq, ITS):
                        add_terms(itq, hq)
                    for w, gw, hw, _, _ in renewed_o(g, b, i):
                        split_lo(pool, w, gw, hw)

            nc.gpsimd.memset(k_t[:, :, BLOCK:BLOCK + SEQ], 0.0).then_inc(zeroed, 1)
            for part in (*pt_hi, *pt_lo):
                nc.gpsimd.memset(part.rearrange("p t h b q -> p (t h b q)").bitcast(F32), 0.0).then_inc(zeroed, 1)
            for w, h in (("q", 0), ("q", 1), ("add", 0), ("q", 2), ("q", 3), ("add", 1), ("o", 0), ("o", 1), ("add", 2), ("o", 2), ("o", 3)):
                if w == "add":
                    add_terms(0, h)
                else:
                    split_lo(pool, w, 0, h)
            walk(pool, KVH, body)


def lora_linear(nc, stack_type, x, norm3, ident, gate_dram, eye_dram, la_dram, lb_dram, as_dram, bs_dram, w_dram, bias_dram, out_dram):
    with stack_type() as stack:
        m = Memory(nc, stack, "p5_")
        GT = TILES // LB
        GTOK = GT * P
        gate, eye = m.sb("gate", [P, NCH, LB]), m.sb("eye", [P, RANK])
        pick = m.sb("pick", [P, NCH, LB, RANK])
        la, lb = m.sb("la", [P, NCH, HIDDEN]), m.sb("lb", [P, NCH, HIDDEN])
        a_all = m.sb("a_all", [P, KC, LB * RANK])
        as_raw = m.sb("as_raw", [P, KC, RANK])
        bs_raw = m.sb("bs_raw", [2 * RANK, HIDDEN])
        a_hi, a_lo = m.sb("a_hi", [P, KC, P], F32R), m.sb("a_lo", [P, KC, P], F32R)
        b_raw = m.sb("b_raw", [RANK, LB, HIDDEN])
        b_hi = [m.sb(f"b_hi{q}", [P, HIDDEN], F32R) for q in range(2)]
        b_lo = [m.sb(f"b_lo{q}", [P, HIDDEN], F32R) for q in range(2)]
        w_raw = m.sb("w_raw", [P, KC, HIDDEN])
        w_hi, w_lo = m.sb("w_hi", [P, KC, HIDDEN], F32R), m.sb("w_lo", [P, KC, HIDDEN], F32R)
        bias = m.sb("bias", [P, HIDDEN])
        xn = [m.sb(f"xn{u}", [P, HIDDEN]) for u in range(2)]
        t_hi = [m.sb(f"t_hi{q}", [P, KC, GTOK], F32R) for q in range(2)]
        t_lo = [m.sb(f"t_lo{q}", [P, KC, GTOK], F32R) for q in range(2)]
        r_hi, r_lo = m.sb("r_hi", [P, GTOK], F32R), m.sb("r_lo", [P, GTOK], F32R)
        y = [m.sb(f"y{u}", [P, HIDDEN]) for u in range(2)]
        yb = [m.sb(f"yb{u}", [P, HIDDEN]) for u in range(2)]
        ps_t = [m.ps(f"ps_t{u}") for u in range(2)]
        ps_y = [m.ps(f"ps_y{u}") for u in range(2)]
        ps_r = m.ps("ps_r")
        ps_a = [m.ps(f"ps_a{i}") for i in range(2)]
        loads = {n: m.sem(n + "_in") for n in ("pick", "la", "lb", "shared", "w")}
        zeroed, picked, w_part, w_ready = m.sem("zeroed"), m.sem("picked"), m.sem("w_part"), m.sem("w_ready")
        a_done, a_copied, bm_done, b_copied = (m.sem(n) for n in ("a_done", "a_copied", "bm_done", "b_copied"))
        shared_hi, shared_ready = m.sem("shared_hi"), m.sem("shared_ready")
        xn_ready, transposed, tile_hi, tile_lo = (m.sem(n) for n in ("xn_ready", "transposed", "tile_hi", "tile_lo"))
        bg_hi, bg_ready = m.sem("bg_hi"), m.sem("bg_ready")
        ag_hi, ag_ready, r_done, rank_hi, rank_lo = (m.sem(n) for n in ("ag_hi", "ag_ready", "r_done", "rank_hi", "rank_lo"))
        y_done, y_added, y_biased = m.sem("y_done"), m.sem("y_added"), m.sem("y_biased")
        stored = [m.sem(f"stored{u}") for u in range(2)]

        def groups(engine, body):
            body(0, 0)
            body(1, 1)
            with engine.Fori(1, LB // 2 - 1) as i:
                body(i * 2, 0)
                body(i * 2 + 1, 1)
            body(LB - 2, 0)
            body(LB - 1, 1)
        block = stack.enter_context(nc.Block())

        @block.sync
        def _(sp):
            for k in range(NPC):
                sp.dma_start(gate[k * RANK:(k + 1) * RANK, :, :], gate_dram[k, :, :].unsqueeze(0).broadcast_to([RANK, NCH, LB])).then_inc(loads["pick"], 16)
            sp.dma_start(eye[:, :], eye_dram).then_inc(loads["pick"], 16)
            sp.dma_start(la[:, :, :], la_dram).then_inc(loads["la"], 16)
            sp.dma_start(lb[:, :, :], lb_dram).then_inc(loads["lb"], 16)
            sp.dma_start(as_raw[:, :, :], as_dram).then_inc(loads["shared"], 16)
            sp.dma_start(bs_raw[RANK:2 * RANK, :], bs_dram).then_inc(loads["shared"], 16)
            sp.dma_start(w_raw[:, :, :], w_dram).then_inc(loads["w"], 16)
            sp.dma_start(bias[:, :], bias_dram.broadcast_to([P, HIDDEN])).then_inc(loads["w"], 16)

            def body(n, q):
                for u in range(GT):
                    t = n * GT + u
                    need(sp, y_biased, t + 1)
                    sp.dma_start(out_dram[:, ds(t, 1), :], yb[u][:, :].unsqueeze(1)).then_inc(stored[u], 16)
            groups(sp, body)
            for u in range(GT):
                sp.wait_ge(stored[u], 16 * LB)

        @block.gpsimd
        def _(pool):
            for part in (*b_hi, *b_lo):
                nc.gpsimd.memset(part[:, :].bitcast(F32), 0.0).then_inc(zeroed, 1)
            pool.wait_ge(loads["w"], 32)

            def body(n, q):
                for u in range(GT):
                    t = n * GT + u
                    need(pool, y_added, t + 1)
                    need(pool, stored[u], n * 16)
                    nc.gpsimd.tensor_tensor(yb[u][:, :], y[u][:, :], bias[:, :], ALU.add).then_inc(y_biased, 1)
            groups(pool, body)

        @block.scalar
        def _(act):
            norm3.finish_scalar(nc, act)
            for c in range(KC):
                act.wait_ge(a_done, c + 1)
                nc.scalar.activation(a_all[:, c, :], ps_a[c % 2][:, 0:LB * RANK], ACT.Copy).then_inc(a_copied, 1)
            act.wait_ge(loads["w"], 32)
            nc.scalar.activation(w_hi[:, :, :], w_raw[:, :, :], ACT.Copy).then_inc(w_part, 1)
            act.wait_ge(zeroed, 6)
            act.wait_ge(loads["shared"], 32)
            nc.scalar.activation(a_hi[:, :, RANK:2 * RANK], as_raw[:, :, :], ACT.Copy).then_inc(shared_hi, 1)
            for q in range(2):
                nc.scalar.activation(b_hi[q][RANK:2 * RANK, :], bs_raw[RANK:2 * RANK, :], ACT.Copy).then_inc(shared_hi, 1)
            act.wait_ge(bm_done, 1)
            for b in range(NPC):
                nc.scalar.activation(b_raw[:, b, :], ps_y[0][b * RANK:(b + 1) * RANK, :], ACT.Copy).then_inc(b_copied, 1)

            def rank_parts(n):
                need(act, r_done, n + 1)
                need(act, y_done, n * GT)
                nc.scalar.activation(r_hi[:, :], ps_r[:, 0:GTOK], ACT.Copy).then_inc(rank_hi, 1)

            def body(n, q):
                for u in range(GT):
                    t = n * GT + u
                    need(act, transposed, t + 1)
                    need(act, y_done, (n - 1) * GT)
                    nc.scalar.activation(t_hi[q][:, :, u * P:(u + 1) * P], ps_t[u][:, :].rearrange("p (c n) -> p c n", c=KC), ACT.Copy).then_inc(tile_hi, 1)
                need(act, r_done, n)
                nc.scalar.activation(a_hi[:, :, 0:RANK], a_all[:, :, ds(n * RANK, RANK)], ACT.Copy).then_inc(ag_hi, 1)
                need(act, y_done, (n - 1) * GT)
                nc.scalar.activation(b_hi[q][0:RANK, :].unsqueeze(1), b_raw[:, ds(n, 1), :], ACT.Copy).then_inc(bg_hi, 1)
                if exists(n - 1, LB):
                    rank_parts(n - 1)
            act.wait_ge(a_copied, KC)
            act.wait_ge(b_copied, LB)
            groups(act, body)
            rank_parts(LB - 1)

        @block.vector
        def _(dve):
            nc.vector.memset(a_hi[:, :, :].bitcast(F32), 0.0).then_inc(zeroed, 1)
            nc.vector.memset(a_lo[:, :, :].bitcast(F32), 0.0).then_inc(zeroed, 1)
            norm3.finish_vector(nc, dve)

            def norm(t, u):
                need(dve, transposed, t - 1)
                norm3.apply(nc, xn[u][:, :], t).then_inc(xn_ready, 1)

            dve.wait_ge(loads["pick"], 16 * (NPC + 1))
            for k in range(NCH):
                nc.vector.tensor_tensor(pick[:, k, :, :], gate[:, k, :].unsqueeze(2).broadcast_to([P, LB, RANK]),
                                        eye[:, :].unsqueeze(1).broadcast_to([P, LB, RANK]), ALU.mult).then_inc(picked, 1)
            for u in range(GT):
                norm(u, u)
            dve.wait_ge(w_part, 1)
            nc.vector.tensor_tensor(w_lo[:, :, :], w_raw[:, :, :], w_hi[:, :, :], ALU.subtract).then_inc(w_ready, 1)
            dve.wait_ge(zeroed, 6)
            dve.wait_ge(shared_hi, 3)
            nc.vector.tensor_tensor(a_lo[:, :, RANK:2 * RANK], as_raw[:, :, :], a_hi[:, :, RANK:2 * RANK], ALU.subtract).then_inc(shared_ready, 1)
            for q in range(2):
                nc.vector.tensor_tensor(b_lo[q][RANK:2 * RANK, :], bs_raw[RANK:2 * RANK, :], b_hi[q][RANK:2 * RANK, :],
                                        ALU.subtract).then_inc(shared_ready, 1)

            dve.wait_ge(bm_done, LB // NPC)
            for b in range(NPC):
                nc.vector.tensor_copy(b_raw[:, NPC + b, :], ps_y[1][b * RANK:(b + 1) * RANK, :]).then_inc(b_copied, 1)

            def rank_parts(n):
                need(dve, rank_hi, n + 1)
                nc.vector.tensor_tensor(r_lo[:, :], ps_r[:, 0:GTOK], r_hi[:, :], ALU.subtract).then_inc(rank_lo, 1)

            def add(n):
                for u in range(GT):
                    t = n * GT + u
                    need(dve, y_done, t + 1)
                    need(dve, y_biased, t - 1)
                    nc.vector.tensor_tensor(y[u][:, :].unsqueeze(1), ps_y[u][:, :].unsqueeze(1), x[:, ds(t, 1), :], ALU.add).then_inc(y_added, 1)

            def body(n, q):
                if not (isinstance(n, int) and n == 0):
                    for u in range(GT):
                        norm(n * GT + u, u)
                for u in range(GT):
                    t = n * GT + u
                    need(dve, tile_hi, t + 1)
                    nc.vector.tensor_tensor(t_lo[q][:, :, u * P:(u + 1) * P], ps_t[u][:, :].rearrange("p (c n) -> p c n", c=KC),
                                            t_hi[q][:, :, u * P:(u + 1) * P], ALU.subtract).then_inc(tile_lo, 1)
                need(dve, ag_hi, n + 1)
                nc.vector.tensor_tensor(a_lo[:, :, 0:RANK], a_all[:, :, ds(n * RANK, RANK)], a_hi[:, :, 0:RANK], ALU.subtract).then_inc(ag_ready, 1)
                need(dve, bg_hi, n + 1)
                nc.vector.tensor_tensor(b_lo[q][0:RANK, :].unsqueeze(1), b_raw[:, ds(n, 1), :], b_hi[q][0:RANK, :].unsqueeze(1),
                                        ALU.subtract).then_inc(bg_ready, 1)
                if exists(n - 1, LB):
                    rank_parts(n - 1)
                    add(n - 1)
            groups(dve, body)
            rank_parts(LB - 1)
            add(LB - 1)

        @block.tensor
        def _(pe):
            def turn_tile(t, u):
                need(pe, xn_ready, t + 1)
                need(pe, tile_lo, t - 1)
                transpose_chunks(nc, ps_t[u], xn[u], ident).then_inc(transposed, 1)

            pe.wait_ge(picked, NCH)
            pe.wait_ge(loads["la"], 16)
            for c in range(KC):
                need(pe, a_copied, c - 1)
                for k in range(NCH):
                    mm = nc.tensor.matmul(ps_a[c % 2][:, 0:LB * RANK], la[:, k, c * P:(c + 1) * P],
                                          pick[:, k, :, :].rearrange("p b r -> p (b r)"), start=(k == 0), stop=(k == NCH - 1))
                mm.then_inc(a_done, 1)
            for u in range(GT):
                turn_tile(u, u)
            pe.wait_ge(loads["lb"], 16)
            for half in range(LB // NPC):
                for k in range(NCH):
                    mm = nc.tensor.matmul(ps_y[half][:, :], pick[:, k, half * NPC:(half + 1) * NPC, :].rearrange("p b r -> p (b r)"),
                                          lb[:, k, :], start=(k == 0), stop=(k == NCH - 1))
                mm.then_inc(bm_done, 1)

            def ranks(n, q):
                need(pe, tile_lo, (n + 1) * GT)
                need(pe, ag_ready, n + 1)
                need(pe, rank_lo, n)
                product3(nc, ps_r[:, 0:GTOK], [(a_hi[:, c, :], a_lo[:, c, :], t_hi[q][:, c, :], t_lo[q][:, c, :])
                                               for c in range(KC)]).then_inc(r_done, 1)

            def linear(n, q):
                for u in range(GT):
                    t, tile = n * GT + u, slice(u * P, (u + 1) * P)
                    need(pe, y_added, t - 1)
                    for c in range(KC):
                        nc.tensor.matmul(ps_y[u][:, :], t_hi[q][:, c, tile], w_hi[:, c, :], start=(c == 0), stop=False)
                        nc.tensor.matmul(ps_y[u][:, :], t_hi[q][:, c, tile], w_lo[:, c, :], start=False, stop=False)
                        nc.tensor.matmul(ps_y[u][:, :], t_lo[q][:, c, tile], w_hi[:, c, :], start=False, stop=False)
                    if u == 0:
                        need(pe, rank_lo, n + 1)
                        need(pe, bg_ready, n + 1)
                    bh, bl = b_hi[q][:, :], b_lo[q][:, :]
                    nc.tensor.matmul(ps_y[u][:, :], r_hi[:, tile], bh, start=False, stop=False)
                    nc.tensor.matmul(ps_y[u][:, :], r_hi[:, tile], bl, start=False, stop=False)
                    nc.tensor.matmul(ps_y[u][:, :], r_lo[:, tile], bh, start=False, stop=True).then_inc(y_done, 1)

            pe.wait_ge(w_ready, 1)
            pe.wait_ge(shared_ready, 3)
            pe.wait_ge(b_copied, LB)

            def body(n, q):
                if not (isinstance(n, int) and n == 0):
                    for u in range(GT):
                        turn_tile(n * GT + u, u)
                if exists(n - 1, LB):
                    linear(n - 1, 1 - q)
                ranks(n, q)
            groups(pe, body)
            linear(LB - 1, 1)


def decoder_layer(nc, stack_type, x, ctx, pos, mask, wq1, wk1, wv1, wo1, wq2, wk2, wv2, wo2, gate, wf, bias, la, lb, las, lbs,
                  ident_c, heads_c, eye_c, table_c, out):
    by_chunk = "(c p) n -> p c n"
    by_tile = "(t p) n -> p t n"
    with stack_type() as stack:
        m = Memory(nc, stack, "")
        k_scr = nc.dram_tensor("k_scratch", (KVH, NB, P, BLOCK), F32, kind="Internal").ap()
        v_scr = nc.dram_tensor("v_scratch", (KVH, NB, P, TPB, D2), F32, kind="Internal").ap()
        cos_scr = nc.dram_tensor("cos_scratch", (P, TOKENS), F32, kind="Internal").ap()
        sin_scr = nc.dram_tensor("sin_scratch", (P, TOKENS), F32, kind="Internal").ap()
        xs, ident = m.sb("x_sb", [P, TILES, HIDDEN]), m.sb("ident", [P, P])
        buffers = (m.sb("stats", [P, TILES, 6]), m.sb("mv", [P, TILES, 2]), m.sb("sd", [P, TILES]), m.sb("rstd", [P, TILES]))
        semaphores = tuple(m.sem("norm_" + n) for n in ("stat", "var", "root", "norm"))
        norm1, norm2, norm3 = (Norm(buffers, semaphores, i) for i in range(3))
        Norm.x = xs
        keys_and_values(nc, stack_type, xs, norm1, ident, x.rearrange(by_tile, p=P), ident_c, pos, table_c, ctx.rearrange(by_chunk, p=P),
                        wk2.rearrange(by_chunk, p=P), wv2.rearrange(by_chunk, p=P), k_scr, v_scr, cos_scr, sin_scr)
        with stack_type() as inner:
            mi = Memory(nc, inner, "a_")
            xt_hi, xt_lo = mi.sb("xt_hi", [P, KC, TOKENS], F32R), mi.sb("xt_lo", [P, KC, TOKENS], F32R)
            v1 = mi.sb("v1", [P, TILES, HIDDEN])
            norm_and_values(nc, stack_type, norm1, xt_hi, xt_lo, v1, ident, wv1.rearrange(by_chunk, p=P))
            self_attention(nc, stack_type, xs, norm2, xt_hi, xt_lo, v1, ident, wq1.rearrange(by_chunk, p=P), wk1.rearrange(by_chunk, p=P), wo1, heads_c)
        with stack_type() as inner:
            mi = Memory(nc, inner, "b_")
            cos_t, sin_t = mi.sb("cos_t", [P, TOKENS]), mi.sb("sin_t", [P, TOKENS])
            bound = mi.sb("bound", [P, BATCH, SEQ])
            xt_hi, xt_lo = mi.sb("xt_hi", [P, KC, TOKENS], F32R), mi.sb("xt_lo", [P, KC, TOKENS], F32R)
            cross_attention(nc, stack_type, xs, norm2, norm3, xt_hi, xt_lo, cos_t, sin_t, bound, ident,
                            mask.rearrange("(b q) k -> q b k", q=SEQ), cos_scr, sin_scr, wq2.rearrange(by_chunk, p=P), wo2, k_scr, v_scr)
        lora_linear(nc, stack_type, xs, norm3, ident, gate, eye_c, la.rearrange("(k q) n -> q k n", q=P), lb.rearrange("(k q) n -> q k n", q=P),
                    las.rearrange(by_chunk, p=P), lbs, wf.rearrange(by_chunk, p=P), bias, out.rearrange(by_tile, p=P))


def rotary_table():
    inv_freq = (np.float32(1.0) / np.power(np.float32(10000.0), np.arange(0, D2, 2, dtype=np.float32) / np.float32(D2))).astype(np.float32)
    angle = np.arange(MAX_POS, dtype=np.float32)[:, None] * inv_freq[None, :]
    cos, sin = np.cos(angle).astype(np.float32), np.sin(angle).astype(np.float32)
    return np.concatenate([cos, cos, sin, -sin], axis=1)


def kernel(**inputs):
    import concourse.bacc as bacc
    from concourse.bass_utils import run_bass_kernel_spmd
    from contextlib import ExitStack

    a = {k: np.asarray(v) for k, v in inputs.items()}
    arrays = {
        "x": a["x"].reshape(TOKENS, HIDDEN),
        "ctx": a["ctx_4096"].reshape(TOKENS, HIDDEN).T,
        "pos": a["pos_BxS2"].reshape(TILES, P).T,
        "mask": a["mask_BxSxS2_ik0"].reshape(TOKENS, SEQ),
        "wq1": a["L0_attn_w_q"].T, "wk1": a["L0_attn_w_k"].T, "wv1": a["L0_attn_w_v"].T, "wo1": a["L0_attn_w_o"].T,
        "wq2": a["L0_xattn_Wq"], "wk2": a["L0_xattn_Wk"], "wv2": a["L0_xattn_Wv"], "wo2": a["L0_xattn_Wo"],
        "gate": a["L0_ffn_gate"].T.reshape(NCH, NPC, LB).transpose(1, 0, 2),
        "wf": a["L0_ffn_kernel"], "bias": a["L0_ffn_bias"].reshape(1, HIDDEN),
        "la": a["L0_ffn_lora_A"].reshape(NLORA * RANK, HIDDEN),
        "lb": a["L0_ffn_lora_B"].transpose(0, 2, 1).reshape(NLORA * RANK, HIDDEN),
        "las": a["L0_ffn_lora_A_shared"].T, "lbs": a["L0_ffn_lora_B_shared"].T,
        "ident_c": np.eye(P, dtype=np.float32),
        "heads_c": np.repeat(np.eye(HPG1, dtype=np.float32), D1, axis=0),
        "eye_c": np.tile(np.eye(RANK, dtype=np.float32), (NPC, 1)),
        "table_c": rotary_table(),
    }
    nc = bacc.Bacc("TRN2", target_bir_lowering=False, num_devices=1)
    given, args = {}, []
    for name, value in arrays.items():
        value = np.ascontiguousarray(value)
        dt = mybir.dt.uint32 if name == "pos" else mybir.dt.from_np(value.dtype)
        if name == "pos":
            value = value.view(np.uint32)
        given["in_" + name] = value
        args.append(nc.dram_tensor("in_" + name, value.shape, dt, kind="ExternalInput").ap())
    args.append(nc.dram_tensor("out", (TOKENS, HIDDEN), F32, kind="ExternalOutput").ap())
    decoder_layer(nc, ExitStack, *args)
    r = run_bass_kernel_spmd(nc, [given], core_ids=[0])
    return r.results[0]["out"].reshape(BATCH, SEQ, HIDDEN)
```
